# Optimizing a Trainium2 kernel written in Bass

```python
import numpy as np
import jax
import jax.numpy as jnp

def _softmax(x, axis=-1):
    return jax.nn.softmax(x, axis=axis)

def _gelu(x):
    return jax.nn.gelu(x, approximate=True)

def _silu(x):
    return jax.nn.silu(x)

def _sigmoid(x):
    return jax.nn.sigmoid(x)

def _layernorm(x, axis=-1, eps=1e-05):
    m = jnp.mean(x, axis=axis, keepdims=True)
    v = jnp.var(x, axis=axis, keepdims=True)
    return (x - m) / jnp.sqrt(v + eps)

def _scatter_add(tgt, idx, src, axis=0):
    return tgt.at[idx].add(src)

def _segment_sum(src, seg, n):
    return jax.ops.segment_sum(src, seg, n)
kernel_name = 'mk_flamingo_gated_d1_seqx_r2_70ffd4'

def setup_inputs(seed: int=0):
    np.random.seed(seed)
    _w = jnp.asarray

    def _rec_inputs():
        import jax
        import jax.numpy as jnp
        _rk = jax.random.key(seed)
        x = 7.22e-05 + 1 * jax.random.normal(jax.random.fold_in(_rk, 1), (2, 2048, 512), jnp.float32)
        _lenS = 2048 - jax.random.randint(jax.random.fold_in(_rk, 7), (2,), 0, max(1, 2048 // 4) + 1, jnp.int32)
        _lenS2 = 128 - jax.random.randint(jax.random.fold_in(_rk, 8), (2,), 0, max(1, 128 // 4) + 1, jnp.int32)
        _ctx_1024P = jax.random.normal(jax.random.fold_in(_rk, 11), (2, 16, 512), jnp.float32)
        _ctx_1024c = jax.random.dirichlet(jax.random.fold_in(_rk, 511), 0.3 * jnp.ones((16,), jnp.float32), (2, 128))
        _ctx_1024t = jnp.einsum('bsk,bkd->bsd', _ctx_1024c, _ctx_1024P)
        _ctx_1024t = _ctx_1024t * jax.lax.rsqrt(jnp.mean(jnp.square(_ctx_1024t)) + 1e-12) * 0.953939
        ctx_1024 = 4.13588e-05 + 0.999923 * (_ctx_1024t + 0.3 * jax.random.normal(jax.random.fold_in(_rk, 611), (2, 128, 512), jnp.float32))
        _g = jax.random.normal(jax.random.fold_in(_rk, 9001), (2, 1), jnp.float32)
        _g = jnp.sign(_g) * jnp.maximum(jnp.abs(_g), 1.0) + (_g == 0) * 1.0
        g_xattn = _g[0]
        g_ffn = _g[1]
        return (x, ctx_1024, g_xattn, g_ffn)
    x, ctx_1024, g_xattn, g_ffn = _rec_inputs()

    def _L0_xattn_setup():
        import jax, jax.numpy as jnp
        import numpy as np
        EMBED_DIM = 512
        NUM_HEADS = 16
        HEAD_DIM = EMBED_DIM // NUM_HEADS
        B, S = (4, 1024)
        key = jax.random.key(seed)
        ks = jax.random.split(key, 11)
        sc = 1.0 / np.sqrt(EMBED_DIM)
        return {'query': jax.random.normal(ks[0], (B, S, EMBED_DIM), jnp.float32), 'key': jax.random.normal(ks[1], (B, S, EMBED_DIM), jnp.float32), 'value': jax.random.normal(ks[2], (B, S, EMBED_DIM), jnp.float32), 'Wq': jax.random.normal(ks[3], (EMBED_DIM, EMBED_DIM), jnp.float32) * sc, 'Wk': jax.random.normal(ks[4], (EMBED_DIM, EMBED_DIM), jnp.float32) * sc, 'Wv': jax.random.normal(ks[5], (EMBED_DIM, EMBED_DIM), jnp.float32) * sc, 'Wo': jax.random.normal(ks[6], (EMBED_DIM, EMBED_DIM), jnp.float32) * sc, 'bq': jax.random.normal(ks[7], (EMBED_DIM,), jnp.float32) * 0.01, 'bk': jax.random.normal(ks[8], (EMBED_DIM,), jnp.float32) * 0.01, 'bv': jax.random.normal(ks[9], (EMBED_DIM,), jnp.float32) * 0.01, 'bo': jax.random.normal(ks[10], (EMBED_DIM,), jnp.float32) * 0.01}
    _L0_xattn_all = _L0_xattn_setup()
    _L0_xattn_in = {k: v for k, v in _L0_xattn_all.items() if k in ('Wq', 'Wk', 'Wv', 'Wo', 'bq', 'bk', 'bv', 'bo')}
    del _L0_xattn_all

    def _L0_ffn_setup():
        import jax, jax.numpy as jnp
        import numpy as np
        import math
        D_IN = 512
        FEATURES = (2048, 2048, 512)
        BATCH, SEQ = (8, 1024)

        def _conn_dense(kernel_bool, x):
            w = jnp.where(kernel_bool, jnp.float32(1.0), jnp.float32(-1.0))
            return x @ w
        key = jax.random.key(seed)
        kx, kk0, kk1, kk2 = jax.random.split(key, 4)
        x = jax.random.normal(kx, (BATCH, SEQ, D_IN), dtype=jnp.float32)
        k0 = jax.random.randint(kk0, (2 * D_IN, FEATURES[0]), 0, 2).astype(jnp.bool_)
        k1 = jax.random.randint(kk1, (FEATURES[0], FEATURES[1]), 0, 2).astype(jnp.bool_)
        k2 = jax.random.randint(kk2, (FEATURES[1], FEATURES[2]), 0, 2).astype(jnp.bool_)
        s0 = jnp.asarray(1.0 / math.sqrt(2 * D_IN), dtype=jnp.float32)
        s1 = jnp.asarray(1.0 / math.sqrt(FEATURES[0]), dtype=jnp.float32)
        s2 = jnp.asarray(1.0 / math.sqrt(FEATURES[1]), dtype=jnp.float32)
        return {'x': x, 'k0': k0, 'k1': k1, 'k2': k2, 's0': s0, 's1': s1, 's2': s2}
    _L0_ffn_all = _L0_ffn_setup()
    _L0_ffn_in = {k: v for k, v in _L0_ffn_all.items() if k in ('k0', 'k1', 'k2', 's0', 's1', 's2')}
    del _L0_ffn_all
    return {'x': x, 'ctx_1024': ctx_1024, 'g_xattn': g_xattn, 'g_ffn': g_ffn, 'L0_xattn_Wq': _L0_xattn_in['Wq'], 'L0_xattn_Wk': _L0_xattn_in['Wk'], 'L0_xattn_Wv': _L0_xattn_in['Wv'], 'L0_xattn_Wo': _L0_xattn_in['Wo'], 'L0_xattn_bq': _L0_xattn_in['bq'], 'L0_xattn_bk': _L0_xattn_in['bk'], 'L0_xattn_bv': _L0_xattn_in['bv'], 'L0_xattn_bo': _L0_xattn_in['bo'], 'L0_ffn_k0': _L0_ffn_in['k0'], 'L0_ffn_k1': _L0_ffn_in['k1'], 'L0_ffn_k2': _L0_ffn_in['k2'], 'L0_ffn_s0': _L0_ffn_in['s0'], 'L0_ffn_s1': _L0_ffn_in['s1'], 'L0_ffn_s2': _L0_ffn_in['s2']}

def reference(x, ctx_1024, g_xattn, g_ffn, L0_xattn_Wq, L0_xattn_Wk, L0_xattn_Wv, L0_xattn_Wo, L0_xattn_bq, L0_xattn_bk, L0_xattn_bv, L0_xattn_bo, L0_ffn_k0, L0_ffn_k1, L0_ffn_k2, L0_ffn_s0, L0_ffn_s1, L0_ffn_s2):
    import jax
    import jax.numpy as jnp

    def _L0_xattn_ref(query, key, value, Wq, Wk, Wv, Wo, bq, bk, bv, bo):
        import jax, jax.numpy as jnp
        import numpy as np
        EMBED_DIM = 512
        NUM_HEADS = 16
        HEAD_DIM = EMBED_DIM // NUM_HEADS
        B, S = (4, 1024)

        def split_heads(x):
            Bx, Sx, _ = x.shape
            return x.reshape(Bx, Sx, NUM_HEADS, HEAD_DIM).transpose(0, 2, 1, 3)
        Q = split_heads(query @ Wq + bq)
        K = split_heads(key @ Wk + bk)
        V = split_heads(value @ Wv + bv)
        scale = 1.0 / np.sqrt(HEAD_DIM).astype(np.float32)
        scores = jnp.einsum('bhqd,bhkd->bhqk', Q, K) * scale
        attn = jax.nn.softmax(scores, axis=-1)
        ctx = jnp.einsum('bhqk,bhkd->bhqd', attn, V)
        ctx = ctx.transpose(0, 2, 1, 3).reshape(query.shape[0], query.shape[1], EMBED_DIM)
        return ctx @ Wo + bo

    def _L0_ffn_ref(x, k0, k1, k2, s0, s1, s2):
        import jax, jax.numpy as jnp
        import numpy as np
        import math
        D_IN = 512
        FEATURES = (2048, 2048, 512)
        BATCH, SEQ = (8, 1024)

        def _conn_dense(kernel_bool, x):
            w = jnp.where(kernel_bool, jnp.float32(1.0), jnp.float32(-1.0))
            return x @ w
        h = jnp.concatenate([x, -x], axis=-1)
        h = s0 * _conn_dense(k0, h)
        h = jax.nn.relu(h) * 2
        h = s1 * _conn_dense(k1, h)
        h = jax.nn.relu(h) * 2
        h = s2 * _conn_dense(k2, h)
        return h
    x = x + jnp.tanh(g_xattn[0]) * _L0_xattn_ref(_layernorm(x, axis=-1), ctx_1024, ctx_1024, L0_xattn_Wq, L0_xattn_Wk, L0_xattn_Wv, L0_xattn_Wo, L0_xattn_bq, L0_xattn_bk, L0_xattn_bv, L0_xattn_bo)
    x = x + jnp.tanh(g_ffn[0]) * _L0_ffn_ref(_layernorm(x, axis=-1), L0_ffn_k0, L0_ffn_k1, L0_ffn_k2, L0_ffn_s0, L0_ffn_s1, L0_ffn_s2)
    return x

_drawn_inputs = setup_inputs


def setup_inputs(seed=0):
    import zlib

    import numpy as np

    out = dict(_drawn_inputs(seed))
    spreads = {}
    factors = {'L0_xattn_bq': 34.259, 'L0_xattn_bk': 64.0, 'L0_xattn_bv': 8.0, 'L0_xattn_bo': 7.74}
    for name, (base, spread) in spreads.items():
        noise = np.random.default_rng([zlib.crc32(name.encode()), seed]).standard_normal(out[name].shape)
        drawn = base * np.exp(spread * noise) if base else spread * noise
        out[name] = jnp.asarray(drawn.astype(out[name].dtype))
    for name, factor in factors.items():
        out[name] = (out[name] * factor).astype(out[name].dtype)
    return out
```

```python
from contextlib import ExitStack

import concourse.bass as bass
from concourse import mybir

P = 128


def gated_block_kernel(nc: bass.Bass, x, ctx, g_xattn, g_ffn, Wq, Wk, Wv, Wo, bq, bk, bv, bo,
                       k0, k1, k2, s0, s1, s2, out):
    f32, f16, f8, u8 = mybir.dt.float32, mybir.dt.float16, mybir.dt.float8e5, mybir.dt.uint8
    ALU = mybir.AluOpType
    ACT = mybir.ActivationFunctionType
    AX = mybir.AxisListType

    TOKENS, D = x.shape
    KEYS_ALL = ctx.shape[0]
    BATCHES = KEYS_ALL // P
    F = k1.shape[0]
    HEAD = 32
    HEADS = D // HEAD
    KT = D // P
    FT = F // P
    G = HEADS // 4
    CHUNK = 512
    TT = CHUNK // P
    CHUNKS = TOKENS // CHUNK
    PER_BATCH = CHUNKS // BATCHES
    U = G * TT
    VW = 2 * HEAD + 2
    EPS = 1e-5
    XS = 64.0
    WS = 256.0
    VS = 16.0
    PS = 1024.0
    W1S = 2.0 ** -11
    OUTS = 4.0 / (XS / 2 * W1S)
    SCALE = HEAD ** -0.5

    SLOTS = [("L0", n, 0) for n in range(FT)]
    for n in range(FT):
        SLOTS += [("L1", n, 0), ("L1", n, 1)] + ([("L2", n - 1, 0)] if n else [])
        SLOTS += [("L1", n, 2), ("L1", n, 3)]
    SLOTS += [("L2", FT - 1, 0)]
    WEAVE = {}

    def weave(slot, *item):
        WEAVE.setdefault(slot, []).append(item)

    FIRST_UNIT = 18
    weave(7, "LN", 0)
    weave(7, "N1", 0)
    weave(7, "N1", 1)
    for t in range(TT):
        weave(8 + t, "T1", t)
        if t + 2 < TT:
            weave(8 + t, "N1", t + 2)
    for g, slot in enumerate((13, 15, 35, 51)):
        weave(slot, "Q", g)
    for u in range(U):
        weave(FIRST_UNIT + 4 * u + 2, "T", u)
        weave(FIRST_UNIT + 4 * u + 4, "PV", u)
    for u in range(U):
        weave(FIRST_UNIT + 4 * u, "S", u)
    for t in range(TT):
        weave(73 + 4 * t, "CT", t)
        weave(75 + 4 * t, "WO", t)
        weave(76 + 4 * t, "N2", t)
        weave(79 + 4 * t, "T2", t)
    LOOP_ITEMS = [item for slot in sorted(WEAVE) for item in WEAVE[slot]]

    FIRST_ITEMS = [("LN", 0), ("N1", 0), ("N1", 1)]
    for t in range(TT):
        FIRST_ITEMS += [("T1", t)] + ([("N1", t + 2)] if t + 2 < TT else [])
    FIRST_ITEMS += [("Q", 0), ("Q", 1)]
    for k in range(U + 2):
        FIRST_ITEMS += [("S", k)] if k < U else []
        FIRST_ITEMS += [("T", k - 1)] if 0 <= k - 1 < U else []
        FIRST_ITEMS += [("PV", k - 2)] if 0 <= k - 2 < U else []
        FIRST_ITEMS += [("Q", k // 4 + 1)] if k in (5, 9) else []
    for t in range(TT + 2):
        FIRST_ITEMS += [("CT", t)] if t < TT else []
        FIRST_ITEMS += [("WO", t - 1)] if 0 <= t - 1 < TT else []
        FIRST_ITEMS += [("N2", t - 2), ("T2", t - 2)] if 0 <= t - 2 < TT else []
    LOOPS = ((0, 1, PER_BATCH - 1), (1, PER_BATCH - 1, CHUNKS - 1))
    ON_PE = ("T1", "Q", "S", "T", "PV", "CT", "WO", "T2")

    LOOP_BANK = {item: 6 + n % 2 for n, item in enumerate(i for i in LOOP_ITEMS if i[0] in ON_PE)}
    KIND_BANKS = {"T1": (6, 7), "Q": (0, 1), "S": (2, 3), "T": (6, 7), "PV": (4, 5),
                  "CT": (0, 1), "WO": (2, 3), "T2": (6, 7)}
    FIRST_BANK = {item: KIND_BANKS[item[0]][item[1] % 2] for item in FIRST_ITEMS if item[0] in ON_PE}

    def user_before(items, bank, item):
        before = [i for i in items[:items.index(item)] if bank.get(i) == bank[item]]
        return before[-1] if before else None

    es = ExitStack()
    with es:
        def sb(name, shape, dt):
            return es.enter_context(nc.sbuf_tensor(name, shape, dt))

        def sem(name):
            return es.enter_context(nc.semaphore(name))

        W0 = sb("W0", [P, KT, F], f8)
        W1 = sb("W1", [P, FT, F], f8)
        W2 = sb("W2", [P, FT, D], f8)
        Wq_hi, Wq_lo = sb("Wq_hi", [P, KT, D], f16), sb("Wq_lo", [P, KT, D], f16)
        Wo_hi, Wo_lo = sb("Wo_hi", [P, KT, D], f16), sb("Wo_lo", [P, KT, D], f16)
        Kst = sb("Kst", [P, HEADS, BATCHES, P], f16)
        V = sb("V", [P, BATCHES, HEADS, VW], f16)
        ident = sb("ident", [P, P], f32)
        scal = sb("scal", [P, 5], f32)
        c = sb("c", [P, 16], f32)
        bq_c, bk_c = sb("bq_c", [P, KT], f32), sb("bk_c", [P, KT], f32)
        bv_b = sb("bv_b", [P, D], f32)
        bo_b = sb("bo_b", [P, D], f32)

        X = sb("X", [P, TT, D], f32)
        RO = sb("RO", [P, 2, TT, D], f32)
        R, O = RO[:, 0], RO[:, 1]
        xn = sb("xn", [P, 2, D], f32)
        xT_hi, xT_lo = sb("xT_hi", [P, KT, CHUNK], f16), sb("xT_lo", [P, KT, CHUNK], f16)
        hT = sb("hT", [P, 2, KT, CHUNK], f16)
        hT_hi, hT_lo = hT[:, 0], hT[:, 1]
        Qf = sb("Qf", [P, CHUNK], f32)
        Qhl = sb("Qhl", [P, 2, 2, CHUNK], f16)
        Qst = sb("Qst", [P, 2, 4, CHUNK], f16)
        Pf = sb("Pf", [P, 2, 4 * P], f32)
        PT_hi, PT_lo = sb("PT_hi", [P, 2, 4 * P], f16), sb("PT_lo", [P, 2, 4 * P], f16)
        pvs = sb("pvs", [P, 2, 4, 2 * HEAD], f32)
        attn = sb("attn", [P, TT, D], f32)
        cT_hi, cT_lo = sb("cT_hi", [P, 2, KT * P], f16), sb("cT_lo", [P, 2, KT * P], f16)
        H0 = sb("H0", [P, 2, FT, CHUNK], f16)
        h0_hi, h0_lo = H0[:, 0], H0[:, 1]
        h1_hi, h1_lo = sb("h1_hi", [P, 2, CHUNK], f16), sb("h1_lo", [P, 2, CHUNK], f16)
        stats = sb("stats", [P, TT, 6], f32)
        mv = sb("mv", [P, TT, 2], f32)
        rstd = sb("rstd", [P, TT], f32)
        var_eps = sb("var_eps", [P, TT], f32)
        minus_one = sb("minus_one", [P, 1], f32)
        halves = sb("halves", [P, 2, TT], f32)
        nmax = sb("nmax", [P, 2, 4], f32)
        rden = sb("rden", [P, 2, 4], f32)

        w1f = W1[:, :, :].rearrange("p k n -> p (k n)").bitcast(f32)
        fw = [w1f[:, w * KT * D:(w + 1) * KT * D].rearrange("p (k n) -> p k n", k=KT) for w in range(4)]
        Wk_f, Wv_f, Wq_f, Wo_f = fw
        k0_u = RO[:, :, :, :].rearrange("p a t d -> p (a t d)").bitcast(u8).rearrange(
            "p (a k n) -> p a k n", a=2, k=KT)
        k1_u = H0[:, :, :, :].rearrange("p a k n -> p (a k n)").bitcast(u8).rearrange(
            "p (k n) -> p k n", k=FT)
        k2_u = hT[:, :, :, :].rearrange("p a k n -> p (a k n)").bitcast(u8).rearrange(
            "p (k n) -> p k n", k=FT)
        attn_f = attn[:, :, :].rearrange("p t d -> p (t d)")
        ctx_f = attn_f[:, 0:BATCHES * D].rearrange("p (b d) -> p b d", b=BATCHES)
        ctxT = attn_f[:, BATCHES * D:2 * BATCHES * D].rearrange("p (k n) -> p k n", k=KT)
        Kf = Pf[:, 0, 0:BATCHES * P]
        KHL = sb("KHL", [P, 2, KT, BATCHES * P], f16)
        Vf = Qf

        banks = [es.enter_context(nc.psum_tensor(f"bank{n}", [P, 512], f32)) for n in range(8)]

        small_in, ctx_in, wk_in, wv_in, wq_in, wo_in = (sem(n) for n in (
            "small_in", "ctx_in", "wk_in", "wv_in", "wq_in", "wo_in"))
        k0_in, k1_in, k2_in = sem("k0_in"), sem("k1_in"), sem("k2_in")
        ident_made, ident_zero, v_ones, half_made, one_made = (
            sem(n) for n in ("ident_made", "ident_zero", "v_ones", "half_made", "one_made"))
        const_tanh, const_step = sem("const_tanh"), sem("const_step")
        ctx_turned, ctx_taken = sem("ctx_turned"), sem("ctx_taken")
        k_done, k_float, k_hi, k_lo, k_stacked = (sem(n) for n in (
            "k_done", "k_float", "k_hi", "k_lo", "k_stacked"))
        v_done, v_float, v_hi, v_lo = (sem(n) for n in ("v_done", "v_float", "v_hi", "v_lo"))
        w_hi, w_lo = sem("w_hi"), sem("w_lo")
        w0_made, w2_made, w1_made = sem("w0_made"), sem("w2_made"), [sem("w1_made0"), sem("w1_made1")]
        x_loaded, r_copied, out_stored = sem("x_loaded"), sem("r_copied"), sem("out_stored")
        var_ready, mv_ready, rstd_ready = sem("var_ready"), sem("mv_ready"), sem("rstd_ready")
        ln_step, xn_ready, xn_turned, xt_hi, xt_lo = (sem(n) for n in (
            "ln_step", "xn_ready", "xn_turned", "xt_hi", "xt_lo"))
        q_done, q_split, q_lo = sem("q_done"), sem("q_split"), sem("q_lo")
        q_stacked = [sem("q_stacked0"), sem("q_stacked1")]
        s_done, s_max, p_ready, p_turned, pt_hi, pt_lo = (sem(n) for n in (
            "s_done", "s_max", "p_ready", "p_turned", "pt_hi", "pt_lo"))
        pv_done, recip_done, pv_scaled, attn_ready = (sem(n) for n in (
            "pv_done", "recip_done", "pv_scaled", "attn_ready"))
        c_turned, ct_hi, ct_lo, wo_done, xb_ready, x1_ready = (sem(n) for n in (
            "c_turned", "ct_hi", "ct_lo", "wo_done", "xb_ready", "x1_ready"))
        ffn_done, ffn_hi, ffn_lo, l2_done, out_ready = (sem(n) for n in (
            "ffn_done", "ffn_hi", "ffn_lo", "l2_done", "out_ready"))

        NX, NU, NT, NG, NF, NLN, NR = 2 * TT, U, TT, G, 2 * FT, 2 * TT, 1 + TT
        STACKS = 16 * 16
        STACK_USES = G // 2

        def nth(chunk, per_chunk, n):
            return chunk * per_chunk + (n + 1)

        tanh_x, tanh_f, _, fin_part, sgn0, sgn1, h_scale, w1_a, w1_b, fin, wo_scale, abs0, abs1 = (
            c[:, n:n + 1] for n in range(13))

        def wait_apart(engine, semaphore, value):
            engine.wait_ge(semaphore, value)
            engine.nop(nofuse=True)

        block = es.enter_context(nc.Block())

        x_v = x.rearrange("(c p t) d -> c p (t d)", p=P, t=TT)
        out_v = out.rearrange("(c p t) d -> c p (t d)", p=P, t=TT)
        X_flat = X[:, :, :].rearrange("p t d -> p (t d)")
        R_flat = R.rearrange("p t d -> p (t d)")
        O_flat = O.rearrange("p t d -> p (t d)")

        @block.sync
        def _(sp):
            sp.dma_start(ctx_f, ctx.rearrange("(b p) d -> p b d", p=P)).then_inc(ctx_in, 16)
            sp.dma_start(Wk_f, Wk.rearrange("(k p) n -> p k n", p=P)).then_inc(wk_in, 16)
            sp.dma_start(X_flat, x_v[0]).then_inc(x_loaded, 16)
            sp.dma_start(Wq_f, Wq.rearrange("(k p) n -> p k n", p=P)).then_inc(wq_in, 16)
            sp.dma_start(Wv_f, Wv.rearrange("(k p) n -> p k n", p=P)).then_inc(wv_in, 16)
            sp.dma_start(Wo_f, Wo.rearrange("(k p) n -> p k n", p=P)).then_inc(wo_in, 16)
            sp.dma_start(k2_u.bitcast(mybir.dt.uint32), k2.rearrange("(k p) n -> p k n", p=P)).then_inc(k2_in, 16)
            for half in range(2):
                sp.dma_start(k0_u[:, half].bitcast(mybir.dt.uint32), k0.rearrange("(a k p) n -> a p k n", a=2, p=P)[half])\
                  .then_inc(k0_in, 16)
            sp.dma_start(k1_u.bitcast(mybir.dt.uint32), k1.rearrange("(k p) n -> p k n", p=P)).then_inc(k1_in, 16)
            sp.wait_ge(k_lo, KT)
            for r in range(4):
                for j in range(4):
                    sp.dma_start(
                        Kst[32 * r:32 * r + 32, j::4, :, :].rearrange("p m b n -> p m (b n)"),
                        KHL[32 * j:32 * j + 32, r // 2, :, :]).then_inc(k_stacked, 16)

            def stack_queries(a, g, first):
                wait_apart(sp, q_lo, nth(a, NG, g))
                if not (first and g < 2):
                    wait_apart(sp, s_done, nth(a, NU, 4 * (g - 2) + 3))
                for r in range(4):
                    for j in range(4):
                        sp.dma_start(Qst[32 * r:32 * r + 32, g % 2, j, :],
                                     Qhl[32 * j:32 * j + 32, g % 2, r % 2, :])\
                          .then_inc(q_stacked[g % 2], 16)

            def keep_x1(a):
                wait_apart(sp, x1_ready, nth(a, NT, NT - 1))
                sp.dma_start(R_flat, X_flat).then_inc(r_copied, 16)

            def load_next(a):
                wait_apart(sp, r_copied, nth(a, 16, 15))
                wait_apart(sp, xn_ready, nth(a, NX, NX - 1))
                sp.dma_start(X_flat, x_v[a + 1]).then_inc(x_loaded, 16)

            def store(f):
                wait_apart(sp, out_ready, nth(f, NT, NT - 1))
                sp.dma_start(out_v[f], O_flat).then_inc(out_stored, 16)

            for g in range(G):
                stack_queries(0, g, True)
            sp.wait_ge(w0_made, KT)
            keep_x1(0)
            load_next(0)
            with sp.Fori(0, CHUNKS - 2) as i:
                for g in range(G):
                    stack_queries(i + 1, g, False)
                store(i)
                keep_x1(i + 1)
                load_next(i + 1)
                wait_apart(sp, out_stored, nth(i, 16, 15))
            for g in range(G):
                stack_queries(CHUNKS - 1, g, False)
            store(CHUNKS - 2)
            keep_x1(CHUNKS - 1)
            sp.wait_ge(out_stored, nth(CHUNKS - 2, 16, 15))
            store(CHUNKS - 1)
            sp.wait_ge(out_stored, nth(CHUNKS - 1, 16, 15))

        @block.gpsimd
        def _(pool):
            pool.memset(ident[:, :], 0.0).then_inc(ident_zero, 1)
            pool.memset(minus_one[:, :], -1.0).then_inc(one_made, 1)
            pool.memset(halves[:, 0, :], -0.5).then_inc(half_made, 1)
            pool.memset(halves[:, 1, :], EPS).then_inc(half_made, 1)
            pool.memset(V[:, :, :, :], 1.0).then_inc(v_ones, 1)
            pool.wait_ge(ident_zero, 1)
            pool.affine_select(out=ident[:, :], in_=ident[:, :], compare_op=ALU.not_equal, fill=1.0,
                               base=0, pattern=[[-1, P]], channel_multiplier=1).then_inc(ident_made, 1)

            def attend(item, a, first):
                kind, n = item
                if kind in ("LN", "WO"):
                    r, w = (0, slice(0, TT)) if kind == "LN" else (1 + n, slice(n, n + 1))
                    pool.wait_ge(mv_ready, nth(a, NR, r))
                    pool.tensor_tensor(var_eps[:, w], mv[:, w, 1], halves[:, 1, w], ALU.add)\
                        .then_inc(var_ready, 1)
                    pool.wait_ge(var_ready, nth(a, NR, r))
                    pool.tensor_tensor(rstd[:, w], var_eps[:, w], halves[:, 0, w], ALU.pow)\
                        .then_inc(rstd_ready, 1)
                if kind == "N1":
                    pool.wait_ge(xn_ready, nth(a, NX, n))
                    pool.tensor_tensor(X[:, n, :], X[:, n, :], bo_b[:, :], ALU.add).then_inc(xb_ready, 1)
                if kind == "PV":
                    g, t = divmod(n, TT)
                    pool.wait_ge(pv_scaled, nth(a, NU, n))
                    pool.tensor_tensor(
                        attn[:, t, g * P:(g + 1) * P].rearrange("p (j d) -> p j d", j=4),
                        pvs[:, n % 2, :, 0:HEAD], pvs[:, n % 2, :, HEAD:2 * HEAD], ALU.add)\
                        .then_inc(attn_ready, 1)

            pool.wait_ge(half_made, 2)
            pool.wait_ge(const_step, 5)
            for item in FIRST_ITEMS:
                attend(item, 0, True)
            for item in LOOP_ITEMS:
                attend(item, 1, False)
            for _, f0, f1 in LOOPS:
                with pool.Fori(f0, f1) as i:
                    for item in LOOP_ITEMS:
                        attend(item, i + 1, False)

        @block.scalar
        def _(act):
            for n, s in enumerate((g_xattn, g_ffn, s0, s1, s2)):
                act.dma_start(scal[:, n:n + 1], s.rearrange("(a n) -> a n", a=1).to_broadcast([P, 1]))\
                   .then_inc(small_in, 16)
            with nc.allow_non_contiguous_dma(reason="two biases of 2 KiB, one feature per row"):
                act.dma_start(bq_c[:, :], bq.rearrange("(k p) -> p k", p=P)).then_inc(small_in, 16)
                act.dma_start(bk_c[:, :], bk.rearrange("(k p) -> p k", p=P)).then_inc(small_in, 16)
            act.dma_start(bv_b[:, :], bv.rearrange("(a n) -> a n", a=1).to_broadcast([P, D]))\
               .then_inc(small_in, 16)
            act.dma_start(bo_b[:, :], bo.rearrange("(a n) -> a n", a=1).to_broadcast([P, D]))\
               .then_inc(small_in, 16)
            act.wait_ge(small_in, 9 * 16)
            act.wait_ge(one_made, 1)
            nc.scalar.activation(c[:, 0:2], scal[:, 0:2], ACT.Tanh).then_inc(const_tanh, 1)
            for m in range(KT):
                act.wait_ge(k_float, m + 1)
                nc.scalar.activation(KHL[:, 0, m, :], Kf, ACT.Copy).then_inc(k_hi, 1)
            act.wait_ge(wq_in, 16)
            nc.scalar.activation(Wq_hi[:, :, :], Wq_f, ACT.Copy, scale=WS).then_inc(w_hi, 1)

            def attend(item, a, first):
                kind, n = item
                if kind in ("T1", "T2"):
                    k = n + (TT if kind == "T2" else 0)
                    bank = (FIRST_BANK if first else LOOP_BANK)[item]
                    dst = xT_hi if kind == "T1" else hT_hi
                    act.wait_ge(xn_turned, nth(a, NX, k))
                    nc.scalar.activation(dst[:, :, n * P:(n + 1) * P],
                                         banks[bank][:, :].rearrange("p (k n) -> p k n", k=KT),
                                         ACT.Copy, scale=XS if kind == "T1" else h_scale)\
                        .then_inc(xt_hi, 1)
                if kind == "Q":
                    bank = banks[(FIRST_BANK if first else LOOP_BANK)[item]]
                    act.wait_ge(q_done, nth(a, NG, n))
                    if not (first and n < 2):
                        act.wait_ge(q_stacked[n % 2], (a * STACK_USES + n // 2) * STACKS)
                    nc.scalar.activation(Qhl[:, n % 2, 0, :], bank[:, :], ACT.Identity,
                                         bias=bq_c[:, n:n + 1], scale=1 / (XS * WS))
                    if not (first and n == 0):
                        act.wait_ge(q_lo, nth(a, NG, n - 1))
                    nc.scalar.activation(Qf[:, :], bank[:, :], ACT.Identity, bias=bq_c[:, n:n + 1],
                                         scale=1 / (XS * WS)).then_inc(q_split, 1)
                if kind == "S":
                    bank = banks[(FIRST_BANK if first else LOOP_BANK)[item]]
                    act.wait_ge(s_max, nth(a, NU, n))
                    for j in range(4):
                        last = nc.scalar.activation(
                            Pf[:, n % 2, j * P:(j + 1) * P], bank[:, j * P:(j + 1) * P], ACT.Exp,
                            bias=nmax[:, n % 2, j:j + 1], scale=1.0)
                    last.then_inc(p_ready, 1)
                if kind == "T":
                    bank = banks[(FIRST_BANK if first else LOOP_BANK)[item]]
                    act.wait_ge(p_turned, nth(a, NU, n))
                    nc.scalar.activation(PT_hi[:, n % 2, :], bank[:, :], ACT.Copy, scale=PS)\
                        .then_inc(pt_hi, 1)
                if kind == "CT":
                    bank = banks[(FIRST_BANK if first else LOOP_BANK)[item]]
                    act.wait_ge(c_turned, nth(a, NT, n))
                    nc.scalar.activation(cT_hi[:, n % 2, :], bank[:, :], ACT.Copy).then_inc(ct_hi, 1)

            def feed(slot, f):
                kind, n, q = slot
                if kind == "L0" or (kind == "L1" and q == 3):
                    e = n + (FT if kind == "L1" else 0)
                    dst = h0_hi[:, n, :] if kind == "L0" else h1_hi[:, n % 2, :]
                    act.wait_ge(ffn_done, nth(f, NF, e))
                    nc.scalar.activation(dst, banks[e % 2][:, :], ACT.Relu).then_inc(ffn_hi, 1)

            for item in FIRST_ITEMS:
                if item == ("Q", 0):
                    for b in range(BATCHES):
                        act.wait_ge(v_float, b + 1)
                        act.wait_ge(v_ones, 1)
                        nc.scalar.activation(V[:, b, :, 0:HEAD],
                                             Vf[:, :].rearrange("p (h d) -> p h d", h=HEADS),
                                             ACT.Copy, scale=VS).then_inc(v_hi, 1)
                    act.wait_ge(wo_in, 16)
                    nc.scalar.activation(Wo_hi[:, :, :], Wo_f, ACT.Copy, scale=WS).then_inc(w_hi, 1)
                    act.wait_ge(v_lo, BATCHES)
                if item[0] == "PV" and item[1] < 4:
                    q = slice(4 * item[1], 4 * item[1] + 4)
                    act.wait_ge(k2_in, 16)
                    nc.scalar.activation(W2[:, q, :], k2_u[:, q, :], ACT.Identity, bias=minus_one[:, :],
                                         scale=2.0, saturate=False).then_inc(w2_made, 1)
                if item == ("T2", 0):
                    act.wait_ge(w2_made, 4)
                attend(item, 0, True)
            act.wait_ge(k1_in, 16)
            act.wait_ge(w_lo, 2)
            act.wait_ge(v_done, BATCHES)
            for s, slot in enumerate(SLOTS):
                if slot[0] == "L0" and slot[1] % 2 == 0:
                    k = slot[1] // 2
                    nc.scalar.activation(W1[:, k, :], k1_u[:, k, :], ACT.Identity, bias=w1_b,
                                         scale=w1_a, saturate=False).then_inc(w1_made[0], 1)
                    act.wait_ge(w1_made[0], k + 1)
                feed(slot, 0)
                for item in WEAVE.get(s, ()):
                    attend(item, 1, False)
            for _, f0, f1 in LOOPS:
                with act.Fori(f0, f1) as i:
                    for s, slot in enumerate(SLOTS):
                        feed(slot, i)
                        for item in WEAVE.get(s, ()):
                            attend(item, i + 1, False)
            for slot in SLOTS:
                feed(slot, CHUNKS - 1)

        @block.vector
        def _(dve):
            V_ = nc.vector
            dve.wait_ge(small_in, 9 * 16)
            V_.tensor_scalar(c[:, 2:4], scal[:, 2:4], 0.0, None, ALU.is_ge).then_inc(const_step, 1)
            dve.wait_ge(const_step, 1)
            V_.tensor_scalar(c[:, 4:6], c[:, 2:4], 2.0, -1.0, ALU.mult, ALU.add).then_inc(const_step, 1)
            dve.wait_ge(const_step, 2)
            dve.wait_ge(const_tanh, 1)
            V_.tensor_scalar(h_scale, sgn0, XS, None, ALU.mult)
            V_.tensor_scalar(w1_a, sgn1, 2 * W1S, None, ALU.mult)
            V_.tensor_scalar(w1_b, sgn1, -W1S, None, ALU.mult)
            V_.tensor_scalar(wo_scale, tanh_x, 1 / (VS * WS), None, ALU.mult)
            V_.tensor_scalar(fin_part, tanh_f, scal[:, 4:5], OUTS, ALU.mult, ALU.mult)
            V_.tensor_tensor(c[:, 11:13], scal[:, 2:4], c[:, 4:6], ALU.mult).then_inc(const_step, 1)
            dve.wait_ge(const_step, 3)
            V_.tensor_scalar(fin, fin_part, abs0, abs1, ALU.mult, ALU.mult)\
                .then_inc(const_step, 1)
            V_.tensor_scalar(bo_b[:, :], bo_b[:, :], tanh_x, None, ALU.mult).then_inc(const_step, 1)
            for b in range(BATCHES):
                dve.wait_ge(ctx_turned, b + 1)
                V_.tensor_copy(ctxT[:, :, b * P:(b + 1) * P],
                               banks[6 + b][:, :].rearrange("p (k n) -> p k n", k=KT))\
                    .then_inc(ctx_taken, 1)
            for m in range(KT):
                dve.wait_ge(k_done, m + 1)
                if m:
                    dve.wait_ge(k_lo, m)
                V_.tensor_scalar(Kf, banks[m][:, 0:BATCHES * P], bk_c[:, m:m + 1], SCALE,
                                 ALU.add, ALU.mult).then_inc(k_float, 1)
                dve.wait_ge(k_hi, m + 1)
                V_.tensor_tensor(KHL[:, 1, m, :], Kf, KHL[:, 0, m, :], ALU.subtract).then_inc(k_lo, 1)

            def make_w0(k):
                V_.tensor_tensor(W0[:, k, :], k0_u[:, 0, k, :], k0_u[:, 1, k, :], ALU.subtract,
                                 saturate=False).then_inc(w0_made, 1)

            def normalise(a, k, src, t, first):
                if not (first and k < 2):
                    dve.wait_ge(xn_turned, nth(a, NX, k - 2))
                V_.tensor_scalar(xn[:, k % 2, :], src, mv[:, t, 0:1], rstd[:, t:t + 1],
                                 ALU.subtract, ALU.mult).then_inc(xn_ready, 1)

            def attend(item, a, first):
                kind, n = item
                bank = banks[(FIRST_BANK if first else LOOP_BANK)[item]] if kind in ON_PE else None
                if kind == "LN":
                    dve.wait_ge(x_loaded, nth(a, 16, 15))
                    for t in range(TT):
                        V_.bn_stats(stats[:, t, :], X[:, t, :]).then_inc(ln_step, 1)
                    wait_apart(dve, ln_step, nth(a, NLN, TT - 1))
                    for t in range(TT):
                        last = V_.bn_aggr(mv[:, t, :], stats[:, t, :])
                    last.then_inc(mv_ready, 1)
                if kind == "N1":
                    if n == 0:
                        dve.wait_ge(rstd_ready, nth(a, NR, 0))
                    normalise(a, n, X[:, n, :], n, first)
                if kind in ("T1", "T2"):
                    k = n + (TT if kind == "T2" else 0)
                    hi, lo = (xT_hi, xT_lo) if kind == "T1" else (hT_hi, hT_lo)
                    dve.wait_ge(xt_hi, nth(a, NX, k))
                    V_.scalar_tensor_tensor(
                        out=lo[:, :, n * P:(n + 1) * P],
                        in0=bank[:, :].rearrange("p (k n) -> p k n", k=KT),
                        scalar=XS if kind == "T1" else h_scale, in1=hi[:, :, n * P:(n + 1) * P],
                        op0=ALU.mult, op1=ALU.subtract).then_inc(xt_lo, 1)
                if kind == "Q":
                    dve.wait_ge(q_split, nth(a, NG, n))
                    V_.tensor_tensor(Qhl[:, n % 2, 1, :], Qf[:, :], Qhl[:, n % 2, 0, :], ALU.subtract)\
                        .then_inc(q_lo, 1)
                if kind == "S":
                    dve.wait_ge(s_done, nth(a, NU, n))
                    V_.tensor_reduce(nmax[:, n % 2, :], bank[:, :].rearrange("p (j k) -> p j k", j=4),
                                     AX.X, ALU.max, negate=True).then_inc(s_max, 1)
                if kind == "T":
                    dve.wait_ge(pt_hi, nth(a, NU, n))
                    V_.scalar_tensor_tensor(out=PT_lo[:, n % 2, :], in0=bank[:, :], scalar=PS,
                                            in1=PT_hi[:, n % 2, :], op0=ALU.mult, op1=ALU.subtract)\
                        .then_inc(pt_lo, 1)
                if kind == "PV":
                    v = bank[:, :].rearrange("p (j n) -> p j n", j=4)
                    dve.wait_ge(pv_done, nth(a, NU, n))
                    if not (first and n < 2):
                        dve.wait_ge(attn_ready, nth(a, NU, n - 2))
                    V_.reciprocal(rden[:, n % 2, :], v[:, :, 2 * HEAD]).then_inc(recip_done, 1)
                    dve.wait_ge(recip_done, nth(a, NU, n))
                    V_.tensor_tensor(
                        pvs[:, n % 2, :, :], v[:, :, 0:2 * HEAD],
                        rden[:, n % 2, :].rearrange("p (j o) -> p j o", o=1).to_broadcast([P, 4, 2 * HEAD]),
                        ALU.mult).then_inc(pv_scaled, 1)
                if kind == "CT":
                    dve.wait_ge(ct_hi, nth(a, NT, n))
                    V_.tensor_tensor(cT_lo[:, n % 2, :], bank[:, :], cT_hi[:, n % 2, :], ALU.subtract)\
                        .then_inc(ct_lo, 1)
                if kind == "WO":
                    dve.wait_ge(wo_done, nth(a, NT, n))
                    dve.wait_ge(xb_ready, nth(a, NT, n))
                    V_.scalar_tensor_tensor(out=X[:, n, :], in0=bank[:, :], scalar=wo_scale,
                                            in1=X[:, n, :], op0=ALU.mult, op1=ALU.add)\
                        .then_inc(x1_ready, 1)
                    dve.wait_ge(x1_ready, nth(a, NT, n))
                    V_.bn_stats(stats[:, n, :], X[:, n, :]).then_inc(ln_step, 1)
                    wait_apart(dve, ln_step, nth(a, NLN, TT + n))
                    V_.bn_aggr(mv[:, n, :], stats[:, n, :]).then_inc(mv_ready, 1)
                if kind == "N2":
                    dve.wait_ge(rstd_ready, nth(a, NR, 1 + n))
                    normalise(a, TT + n, X[:, n, :], n, first)

            def feed(slot, f):
                kind, n, q = slot
                if kind == "L0" or (kind == "L1" and q == 3):
                    e = n + (FT if kind == "L1" else 0)
                    hi, lo = (h0_hi[:, n, :], h0_lo[:, n, :]) if kind == "L0" else (
                        h1_hi[:, n % 2, :], h1_lo[:, n % 2, :])
                    dve.wait_ge(ffn_hi, nth(f, NF, e))
                    V_.scalar_tensor_tensor(out=lo, in0=banks[e % 2][:, :], scalar=0.0, in1=hi,
                                            op0=ALU.max, op1=ALU.subtract).then_inc(ffn_lo, 1)
                if kind == "L2" and n == FT - 1:
                    dve.wait_ge(r_copied, nth(f, 16, 15))
                    for t in range(TT):
                        dve.wait_ge(l2_done, nth(f, NT, t))
                        V_.scalar_tensor_tensor(out=O[:, t, :], in0=banks[2 + t][:, :], scalar=fin,
                                                in1=R[:, t, :], op0=ALU.mult, op1=ALU.add)\
                            .then_inc(out_ready, 1)

            for item in FIRST_ITEMS:
                if item == ("Q", 0):
                    dve.wait_ge(w_hi, 1)
                    V_.scalar_tensor_tensor(out=Wq_lo[:, :, :].rearrange("p k n -> p (k n)"),
                                            in0=Wq_f.rearrange("p k n -> p (k n)"), scalar=WS,
                                            in1=Wq_hi[:, :, :].rearrange("p k n -> p (k n)"),
                                            op0=ALU.mult, op1=ALU.subtract).then_inc(w_lo, 1)
                    for b in range(BATCHES):
                        dve.wait_ge(v_done, b + 1)
                        if b:
                            dve.wait_ge(v_lo, b)
                        V_.tensor_tensor(Vf[:, :], banks[4 + b][:, :], bv_b[:, :], ALU.add)\
                            .then_inc(v_float, 1)
                        dve.wait_ge(v_hi, b + 1)
                        V_.scalar_tensor_tensor(
                            out=V[:, b, :, HEAD:2 * HEAD], in0=Vf[:, :].rearrange("p (h d) -> p h d", h=HEADS),
                            scalar=VS, in1=V[:, b, :, 0:HEAD], op0=ALU.mult, op1=ALU.subtract)\
                            .then_inc(v_lo, 1)
                    dve.wait_ge(w_hi, 2)
                    V_.scalar_tensor_tensor(out=Wo_lo[:, :, :].rearrange("p k n -> p (k n)"),
                                            in0=Wo_f.rearrange("p k n -> p (k n)"), scalar=WS,
                                            in1=Wo_hi[:, :, :].rearrange("p k n -> p (k n)"),
                                            op0=ALU.mult, op1=ALU.subtract).then_inc(w_lo, 1)
                if item == ("S", 4):
                    dve.wait_ge(k0_in, 32)
                if item[0] == "S" and item[1] in (4, 7, 10, 13):
                    make_w0(item[1] // 3 - 1)
                if item == ("T2", 0):
                    dve.wait_ge(w2_made, 4)
                attend(item, 0, True)
            dve.wait_ge(k1_in, 16)
            for s, slot in enumerate(SLOTS):
                if slot[0] == "L0" and slot[1] % 2 == 0:
                    k = FT // 2 + slot[1] // 2
                    V_.tensor_scalar(W1[:, k, :], k1_u[:, k, :], w1_a, w1_b, ALU.mult, ALU.add,
                                     saturate=False).then_inc(w1_made[1], 1)
                    dve.wait_ge(w1_made[1], slot[1] // 2 + 1)
                feed(slot, 0)
                for item in WEAVE.get(s, ()):
                    attend(item, 1, False)
            for _, f0, f1 in LOOPS:
                with dve.Fori(f0, f1) as i:
                    for s, slot in enumerate(SLOTS):
                        feed(slot, i)
                        for item in WEAVE.get(s, ()):
                            attend(item, i + 1, False)
            for slot in SLOTS:
                feed(slot, CHUNKS - 1)

        @block.tensor
        def _(pe):
            mm, turn = nc.tensor.matmul, nc.tensor.transpose
            pe.wait_ge(ident_made, 1)
            pe.wait_ge(ctx_in, 16)
            for b in range(BATCHES):
                for k in range(KT):
                    last = turn(banks[6 + b][:, k * P:(k + 1) * P], ctx_f[:, b, k * P:(k + 1) * P],
                                ident[:, :])
                last.then_inc(ctx_turned, 1)
            pe.wait_ge(ctx_taken, BATCHES)
            pe.wait_ge(wk_in, 16)
            for m in range(KT):
                for k in range(KT):
                    last = mm(banks[m][:, 0:BATCHES * P], Wk_f[:, k, m * P:(m + 1) * P], ctxT[:, k, :],
                              start=k == 0, stop=k == KT - 1)
                last.then_inc(k_done, 1)
            pe.wait_ge(wv_in, 16)
            for b in range(BATCHES):
                for k in range(KT):
                    last = mm(banks[4 + b][:, :], ctxT[:, k, b * P:(b + 1) * P], Wv_f[:, k, :],
                              start=k == 0, stop=k == KT - 1)
                last.then_inc(v_done, 1)

            def released(item, a):
                kind, n = item
                return {"T1": (xt_lo, NX, n), "T2": (xt_lo, NX, TT + n), "Q": (q_split, NG, n),
                        "S": (p_ready, NU, n), "T": (pt_lo, NU, n), "PV": (pv_scaled, NU, n),
                        "CT": (ct_lo, NT, n), "WO": (x1_ready, NT, n)}[kind]

            def attend(item, a, batch, first):
                kind, n = item
                if kind not in ON_PE:
                    return
                if first:
                    bank, before, since = FIRST_BANK[item], user_before(FIRST_ITEMS, FIRST_BANK, item), a
                else:
                    bank, before, since = LOOP_BANK[item], user_before(LOOP_ITEMS, LOOP_BANK, item), a
                    if before is None:
                        before, since = [i for i in LOOP_ITEMS if LOOP_BANK.get(i) == bank][-1], a - 1
                if before is not None:
                    signal, per_chunk, m = released(before, a)
                    pe.wait_ge(signal, nth(since, per_chunk, m))
                bank = banks[bank]
                if kind in ("T1", "T2"):
                    k = n + (TT if kind == "T2" else 0)
                    pe.wait_ge(xn_ready, nth(a, NX, k))
                    for d in range(KT):
                        last = turn(bank[:, d * P:(d + 1) * P], xn[:, k % 2, d * P:(d + 1) * P],
                                    ident[:, :])
                    last.then_inc(xn_turned, 1)
                if kind == "Q":
                    if n == 0:
                        pe.wait_ge(xt_lo, nth(a, NX, TT - 1))
                    for k in range(KT):
                        w_h, w_l = (w[:, k, n * P:(n + 1) * P] for w in (Wq_hi, Wq_lo))
                        mm(bank[:, :], w_h, xT_hi[:, k, :], start=k == 0, stop=False)
                        mm(bank[:, :], w_h, xT_lo[:, k, :], start=False, stop=False)
                        last = mm(bank[:, :], w_l, xT_hi[:, k, :], start=False, stop=k == KT - 1)
                    last.then_inc(q_done, 1)
                if kind == "S":
                    g, t = divmod(n, TT)
                    if t == 0:
                        pe.wait_ge(q_stacked[g % 2], (a * STACK_USES + g // 2 + 1) * STACKS)
                    for j in range(4):
                        last = mm(bank[:, j * P:(j + 1) * P], Qst[:, g % 2, j, t * P:(t + 1) * P],
                                  Kst[:, 4 * g + j, batch, :], start=True, stop=True)
                    last.then_inc(s_done, 1)
                if kind == "T":
                    pe.wait_ge(p_ready, nth(a, NU, n))
                    for j in range(4):
                        last = turn(bank[:, j * P:(j + 1) * P], Pf[:, n % 2, j * P:(j + 1) * P],
                                    ident[:, :])
                    last.then_inc(p_turned, 1)
                if kind == "PV":
                    g, t = divmod(n, TT)
                    pe.wait_ge(pt_lo, nth(a, NU, n))
                    for j in range(4):
                        o, v = bank[:, j * P:j * P + VW - 1], V[:, batch, 4 * g + j, 0:VW - 1]
                        mm(o, PT_hi[:, n % 2, j * P:(j + 1) * P], v, start=True, stop=False)
                        last = mm(o, PT_lo[:, n % 2, j * P:(j + 1) * P], v, start=False, stop=True)
                    last.then_inc(pv_done, 1)
                if kind == "CT":
                    pe.wait_ge(attn_ready, nth(a, NU, (G - 1) * TT + n))
                    for k in range(KT):
                        last = turn(bank[:, k * P:(k + 1) * P], attn[:, n, k * P:(k + 1) * P],
                                    ident[:, :])
                    last.then_inc(c_turned, 1)
                if kind == "WO":
                    pe.wait_ge(ct_lo, nth(a, NT, n))
                    for k in range(KT):
                        c_h, c_l = (w[:, n % 2, k * P:(k + 1) * P] for w in (cT_hi, cT_lo))
                        mm(bank[:, :], c_h, Wo_hi[:, k, :], start=k == 0, stop=False)
                        mm(bank[:, :], c_h, Wo_lo[:, k, :], start=False, stop=False)
                        last = mm(bank[:, :], c_l, Wo_hi[:, k, :], start=False, stop=k == KT - 1)
                    last.then_inc(wo_done, 1)

            def feed(slot, f):
                kind, n, q = slot
                if kind == "L0":
                    if n == 0:
                        wait_apart(pe, xt_lo, nth(f, NX, NX - 1))
                    if n >= 2:
                        wait_apart(pe, ffn_lo, nth(f, NF, n - 2))
                    for k in range(KT):
                        w = W0[:, k, n * P:(n + 1) * P]
                        mm(banks[n % 2][:, :], w, hT_hi[:, k, :], start=k == 0, stop=False)
                        last = mm(banks[n % 2][:, :], w, hT_lo[:, k, :], start=False, stop=k == KT - 1)
                    last.then_inc(ffn_done, 1)
                if kind == "L1":
                    if q == 0:
                        wait_apart(pe, ffn_lo, nth(f, NF, FT + n - 2))
                    if n == 0:
                        wait_apart(pe, ffn_lo, nth(f, NF, 4 * q + 3))
                    for k in range(4 * q, 4 * q + 4):
                        w = W1[:, k, n * P:(n + 1) * P]
                        mm(banks[n % 2][:, :], w, h0_hi[:, k, :], start=k == 0, stop=False)
                        last = mm(banks[n % 2][:, :], w, h0_lo[:, k, :], start=False, stop=k == FT - 1)
                    if q == 3:
                        last.then_inc(ffn_done, 1)
                if kind == "L2":
                    wait_apart(pe, ffn_lo, nth(f, NF, FT + n))
                    for t in range(TT):
                        tok = slice(t * P, (t + 1) * P)
                        mm(banks[2 + t][:, :], h1_hi[:, n % 2, tok], W2[:, n, :],
                           start=n == 0, stop=False)
                        last = mm(banks[2 + t][:, :], h1_lo[:, n % 2, tok], W2[:, n, :],
                                  start=False, stop=n == FT - 1)
                        if n == FT - 1:
                            last.then_inc(l2_done, 1)

            for item in FIRST_ITEMS:
                if item == ("Q", 0):
                    pe.wait_ge(w_lo, 1)
                    pe.wait_ge(k_lo, KT)
                if item == ("S", 0):
                    pe.wait_ge(k_stacked, 16 * 16)
                if item == ("PV", 0):
                    pe.wait_ge(v_lo, BATCHES)
                if item == ("WO", 0):
                    pe.wait_ge(w_lo, 2)
                attend(item, 0, 0, True)
            pe.wait_ge(w0_made, KT)
            pe.wait_ge(w2_made, 4)
            for s, slot in enumerate(SLOTS):
                if slot[:2] == ("L1", 0):
                    pe.wait_ge(w1_made[slot[2] // 2], 4 * (slot[2] % 2) + 4)
                feed(slot, 0)
                for item in WEAVE.get(s, ()):
                    attend(item, 1, 0, False)
            for batch, f0, f1 in LOOPS:
                with pe.Fori(f0, f1) as i:
                    for s, slot in enumerate(SLOTS):
                        feed(slot, i)
                        for item in WEAVE.get(s, ()):
                            attend(item, i + 1, batch, False)
            for slot in SLOTS:
                feed(slot, CHUNKS - 1)


_INS = ["x", "ctx_1024", "g_xattn", "g_ffn", "L0_xattn_Wq", "L0_xattn_Wk", "L0_xattn_Wv", "L0_xattn_Wo",
        "L0_xattn_bq", "L0_xattn_bk", "L0_xattn_bv", "L0_xattn_bo", "L0_ffn_k0", "L0_ffn_k1",
        "L0_ffn_k2", "L0_ffn_s0", "L0_ffn_s1", "L0_ffn_s2"]


def kernel(**inputs):
    import numpy as _np
    import concourse.bacc as _bacc
    from concourse import mybir as _mybir
    from concourse.bass_utils import run_bass_kernel_spmd as _run

    nc = _bacc.Bacc("TRN2", target_bir_lowering=False, num_devices=1)
    arrays, args = {}, []
    for name in _INS:
        a = _np.ascontiguousarray(inputs[name])
        if a.ndim == 3:
            a = a.reshape(-1, a.shape[-1])
        if a.ndim == 0:
            a = a.reshape(1)
        if a.dtype == _np.bool_:
            a = a.view(_np.uint32)
        arrays[f"in_{name}_dram"] = a
        args.append(nc.dram_tensor(f"in_{name}_dram", a.shape, _mybir.dt.from_np(a.dtype),
                                   kind="ExternalInput").ap())
    shape = inputs["x"].shape
    out = nc.dram_tensor("out_dram", (shape[0] * shape[1], shape[2]), _mybir.dt.float32,
                         kind="ExternalOutput").ap()
    gated_block_kernel(nc, *args, out)
    r = _run(nc, [arrays], core_ids=[0])
    return r.results[0]["out_dram"].reshape(shape)
```

```python
from contextlib import ExitStack

import concourse.bass as bass
from concourse import mybir

P = 128


def gated_block_kernel(nc: bass.Bass, x, ctx, g_xattn, g_ffn, Wq, Wk, Wv, Wo, bq, bk, bv, bo,
                       k0, k1, k2, s0, s1, s2, out):
    f32, f16, f8, u8 = mybir.dt.float32, mybir.dt.float16, mybir.dt.float8e5, mybir.dt.uint8
    ALU = mybir.AluOpType
    ACT = mybir.ActivationFunctionType
    AX = mybir.AxisListType

    TOKENS, D = x.shape
    KEYS_ALL = ctx.shape[0]
    BATCHES = KEYS_ALL // P
    F = k1.shape[0]
    HEAD = 32
    HEADS = D // HEAD
    KT = D // P
    FT = F // P
    G = HEADS // 4
    CHUNK = 512
    TT = CHUNK // P
    CHUNKS = TOKENS // CHUNK
    PER_BATCH = CHUNKS // BATCHES
    U = G * TT
    VW = 2 * HEAD + 2
    EPS = 1e-5
    XS = 64.0
    WS = 256.0
    VS = 16.0
    PS = 1024.0
    W1S = 2.0 ** -11
    OUTS = 4.0 / (XS / 2 * W1S)
    SCALE = HEAD ** -0.5

    SLOTS = [("L0", n, 0) for n in range(FT)]
    for n in range(FT):
        SLOTS += [("L1", n, 0), ("L1", n, 1)] + ([("L2", n - 1, 0)] if 0 < n < FT - 1 else [])
        SLOTS += [("L1", n, 2), ("L1", n, 3)]
    SLOTS += [("L2", FT - 2, 0), ("L2", FT - 1, 0)]
    WEAVE = {}

    def weave(slot, *item):
        WEAVE.setdefault(slot, []).append(item)

    FIRST_UNIT = 15
    weave(1, "LN", 0)
    weave(2, "N1", 0)
    weave(2, "N1", 1)
    for t in range(TT):
        weave(4 + t, "T1", t)
        if t + 2 < TT:
            weave(4 + t, "N1", t + 2)
    for g, slot in enumerate((9, 11, FIRST_UNIT + 17, FIRST_UNIT + 33)):
        weave(slot, "Q", g)
    for u in range(U):
        weave(FIRST_UNIT + 4 * u + 2, "T", u)
        weave(FIRST_UNIT + 4 * u + 4, "PV", u)
    for u in range(U):
        weave(FIRST_UNIT + 4 * u, "S", u)
    for t in range(TT):
        weave(FIRST_UNIT + 55 + 4 * t, "CT", t)
        weave(FIRST_UNIT + 57 + 4 * t, "WO", t)
        weave(FIRST_UNIT + 58 + 4 * t, "N2", t)
        weave(FIRST_UNIT + 61 + 4 * t, "T2", t)
    LOOP_ITEMS = [item for slot in sorted(WEAVE) for item in WEAVE[slot]]

    FIRST_ITEMS = [("LN", 0), ("N1", 0), ("N1", 1)]
    for t in range(TT):
        FIRST_ITEMS += [("T1", t)] + ([("N1", t + 2)] if t + 2 < TT else [])
    FIRST_ITEMS += [("Q", 0), ("Q", 1)]
    for k in range(U + 2):
        FIRST_ITEMS += [("S", k)] if k < U else []
        FIRST_ITEMS += [("T", k - 1)] if 0 <= k - 1 < U else []
        FIRST_ITEMS += [("PV", k - 2)] if 0 <= k - 2 < U else []
        FIRST_ITEMS += [("Q", k // 4 + 1)] if k in (5, 9) else []
    for t in range(TT + 2):
        FIRST_ITEMS += [("CT", t)] if t < TT else []
        FIRST_ITEMS += [("WO", t - 1)] if 0 <= t - 1 < TT else []
        FIRST_ITEMS += [("N2", t - 2), ("T2", t - 2)] if 0 <= t - 2 < TT else []
    LOOPS = ((0, 1, PER_BATCH - 1), (1, PER_BATCH - 1, CHUNKS - 1))
    ON_PE = ("T1", "Q", "S", "T", "PV", "CT", "WO", "T2")

    LOOP_BANK = {item: 6 + n % 2 for n, item in enumerate(i for i in LOOP_ITEMS if i[0] in ON_PE)}
    KIND_BANKS = {"T1": (6, 7), "Q": (0, 1), "S": (2, 3), "T": (6, 7), "PV": (4, 5),
                  "CT": (0, 1), "WO": (2, 3), "T2": (6, 7)}
    FIRST_BANK = {item: KIND_BANKS[item[0]][item[1] % 2] for item in FIRST_ITEMS if item[0] in ON_PE}

    def user_before(items, bank, item):
        before = [i for i in items[:items.index(item)] if bank.get(i) == bank[item]]
        return before[-1] if before else None

    es = ExitStack()
    with es:
        def sb(name, shape, dt):
            return es.enter_context(nc.sbuf_tensor(name, shape, dt))

        def sem(name):
            return es.enter_context(nc.semaphore(name))

        W0 = sb("W0", [P, KT, F], f8)
        W1 = sb("W1", [P, FT, F], f8)
        W2 = sb("W2", [P, FT, D], f8)
        Wq_hi, Wq_lo = sb("Wq_hi", [P, KT, D], f16), sb("Wq_lo", [P, KT, D], f16)
        Wo_hi, Wo_lo = sb("Wo_hi", [P, KT, D], f16), sb("Wo_lo", [P, KT, D], f16)
        Kst = sb("Kst", [P, HEADS, BATCHES, P], f16)
        V = sb("V", [P, BATCHES, HEADS, VW], f16)
        ident = sb("ident", [P, P], f32)
        scal = sb("scal", [P, 5], f32)
        c = sb("c", [P, 16], f32)
        bq_c, bk_c = sb("bq_c", [P, KT], f32), sb("bk_c", [P, KT], f32)
        bv_b = sb("bv_b", [P, D], f32)
        bo_b = sb("bo_b", [P, D], f32)

        Y = sb("Y", [P, TT, D], f32)
        XR = sb("XR", [P, 2, TT, D], f32)
        X, R = XR[:, 0], XR[:, 1]
        xn = sb("xn", [P, 2, D], f32)
        xT_hi, xT_lo = sb("xT_hi", [P, KT, CHUNK], f16), sb("xT_lo", [P, KT, CHUNK], f16)
        hT = sb("hT", [P, 2, KT, CHUNK], f16)
        hT_hi, hT_lo = hT[:, 0], hT[:, 1]
        Qf = sb("Qf", [P, CHUNK], f32)
        Qhl = sb("Qhl", [P, 2, 2, CHUNK], f16)
        Qst = sb("Qst", [P, 2, 4, CHUNK], f16)
        Pf = sb("Pf", [P, 2, 4 * P], f32)
        PT_hi, PT_lo = sb("PT_hi", [P, 2, 4 * P], f16), sb("PT_lo", [P, 2, 4 * P], f16)
        pvs = sb("pvs", [P, 2, 4, 2 * HEAD], f32)
        attn = sb("attn", [P, TT, D], f32)
        cT_hi, cT_lo = sb("cT_hi", [P, 2, KT * P], f16), sb("cT_lo", [P, 2, KT * P], f16)
        H0 = sb("H0", [P, 2, FT, CHUNK], f16)
        h0_hi, h0_lo = H0[:, 0], H0[:, 1]
        h1_hi, h1_lo = sb("h1_hi", [P, 2, CHUNK], f16), sb("h1_lo", [P, 2, CHUNK], f16)
        stats = sb("stats", [P, TT, 6], f32)
        mv = sb("mv", [P, TT, 2], f32)
        rstd = sb("rstd", [P, TT], f32)
        var_eps = sb("var_eps", [P, TT], f32)
        minus_one = sb("minus_one", [P, 1], f32)
        halves = sb("halves", [P, 2, TT], f32)
        nmax = sb("nmax", [P, 2, 4], f32)
        rden = sb("rden", [P, 2, 4], f32)

        w1f = W1[:, :, :].rearrange("p k n -> p (k n)").bitcast(f32)
        fw = [w1f[:, w * KT * D:(w + 1) * KT * D].rearrange("p (k n) -> p k n", k=KT) for w in range(4)]
        Wk_f, Wv_f, Wq_f, Wo_f = fw
        k0_u = XR[:, :, :, :].rearrange("p a t d -> p (a t d)").bitcast(u8).rearrange(
            "p (a k n) -> p a k n", a=2, k=KT)
        k1_u = H0[:, :, :, :].rearrange("p a k n -> p (a k n)").bitcast(u8).rearrange(
            "p (k n) -> p k n", k=FT)
        k2_u = hT[:, :, :, :].rearrange("p a k n -> p (a k n)").bitcast(u8).rearrange(
            "p (k n) -> p k n", k=FT)
        attn_f = attn[:, :, :].rearrange("p t d -> p (t d)")
        ctx_f = attn_f[:, 0:BATCHES * D].rearrange("p (b d) -> p b d", b=BATCHES)
        ctxT = attn_f[:, BATCHES * D:2 * BATCHES * D].rearrange("p (k n) -> p k n", k=KT)
        Kf = [Pf[:, n, 0:BATCHES * P] for n in range(2)]
        KHL = sb("KHL", [P, 2, KT, BATCHES * P], f16)
        Vf = [pvs[:, :, :, :].rearrange("p a j n -> p (a j n)"),
              h1_hi[:, :, :].rearrange("p a n -> p (a n)").bitcast(f32)]

        banks = [es.enter_context(nc.psum_tensor(f"bank{n}", [P, 512], f32)) for n in range(8)]

        scalars_in, bq_in, bk_in, bv_in, bo_in, ctx_in, wk_in, wv_in, wq_in, wo_in = (sem(n) for n in (
            "scalars_in", "bq_in", "bk_in", "bv_in", "bo_in", "ctx_in", "wk_in", "wv_in", "wq_in", "wo_in"))
        k0_in, k1_in, k2_in = sem("k0_in"), sem("k1_in"), sem("k2_in")
        ident_made, ident_zero, v_ones, half_made, one_made = (
            sem(n) for n in ("ident_made", "ident_zero", "v_ones", "half_made", "one_made"))
        const_tanh, const_step = sem("const_tanh"), sem("const_step")
        ctx_turned, ctx_taken = sem("ctx_turned"), sem("ctx_taken")
        k_done, k_float, k_hi, k_lo, k_stacked = (sem(n) for n in (
            "k_done", "k_float", "k_hi", "k_lo", "k_stacked"))
        k_zero, k_spread = sem("k_zero"), sem("k_spread")
        v_done, v_float, v_hi, v_lo = (sem(n) for n in ("v_done", "v_float", "v_hi", "v_lo"))
        w_hi, w_lo = sem("w_hi"), sem("w_lo")
        w0_made, w2_made, w1_made = sem("w0_made"), sem("w2_made"), [sem("w1_made0"), sem("w1_made1")]
        x_loaded, r_copied, out_stored = sem("x_loaded"), sem("r_copied"), sem("out_stored")
        var_ready, mv_ready, rstd_ready = sem("var_ready"), sem("mv_ready"), sem("rstd_ready")
        ln_step, xn_ready, xn_turned, xt_hi, xt_lo = (sem(n) for n in (
            "ln_step", "xn_ready", "xn_turned", "xt_hi", "xt_lo"))
        q_done, q_split, q_lo = sem("q_done"), sem("q_split"), sem("q_lo")
        q_stacked = [sem("q_stacked0"), sem("q_stacked1")]
        s_done, s_max, p_ready, p_turned, pt_hi, pt_lo = (sem(n) for n in (
            "s_done", "s_max", "p_ready", "p_turned", "pt_hi", "pt_lo"))
        pv_done, recip_done, pv_scaled, attn_ready = (sem(n) for n in (
            "pv_done", "recip_done", "pv_scaled", "attn_ready"))
        c_turned, ct_hi, ct_lo, wo_done, xb_ready, x1_ready = (sem(n) for n in (
            "c_turned", "ct_hi", "ct_lo", "wo_done", "xb_ready", "x1_ready"))
        ffn_done, ffn_hi, ffn_lo, l2_done, out_ready = (sem(n) for n in (
            "ffn_done", "ffn_hi", "ffn_lo", "l2_done", "out_ready"))

        NX, NU, NT, NG, NF, NLN, NR = 2 * TT, U, TT, G, 2 * FT, 2 * TT, 1 + TT
        STACKS = 16 * 16
        STACK_USES = G // 2

        def nth(chunk, per_chunk, n):
            return chunk * per_chunk + (n + 1)

        tanh_x, tanh_f, _, fin_part, sgn0, sgn1, h_scale, w1_a, w1_b, fin, wo_scale, abs0, abs1 = (
            c[:, n:n + 1] for n in range(13))

        def wait_apart(engine, semaphore, value):
            engine.wait_ge(semaphore, value)
            engine.nop(nofuse=True)

        block = es.enter_context(nc.Block())

        x_v = x.rearrange("(c p t) d -> c p (t d)", p=P, t=TT)
        out_v = out.rearrange("(c p t) d -> c p (t d)", p=P, t=TT)
        Y_flat = Y[:, :, :].rearrange("p t d -> p (t d)")
        X_flat = X.rearrange("p t d -> p (t d)")
        R_flat = R.rearrange("p t d -> p (t d)")

        @block.sync
        def _(sp):
            def load(to, source, semaphore):
                sp.dma_start(to, source).then_inc(semaphore, 16)

            def by_rows(w):
                return w.rearrange("(k p) n -> p k n", p=P)

            def to_all(v, n):
                return v.rearrange("(a n) -> a n", a=1).to_broadcast([P, n])

            load(ctx_f, ctx.rearrange("(b p) d -> p b d", p=P), ctx_in)
            load(Wk_f, by_rows(Wk), wk_in)
            with nc.allow_non_contiguous_dma(reason="two biases of 2 KiB, one feature per row"):
                load(bk_c[:, :], bk.rearrange("(k p) -> p k", p=P), bk_in)
                load(Y_flat, x_v[0], x_loaded)
                load(Wq_f, by_rows(Wq), wq_in)
                load(bq_c[:, :], bq.rearrange("(k p) -> p k", p=P), bq_in)
            load(Wv_f, by_rows(Wv), wv_in)
            load(bv_b[:, :], to_all(bv, D), bv_in)
            for n, s in enumerate((g_xattn, g_ffn, s0, s1, s2)):
                load(scal[:, n:n + 1], to_all(s, 1), scalars_in)
            load(bo_b[:, :], to_all(bo, D), bo_in)
            load(Wo_f, by_rows(Wo), wo_in)
            for half in range(2):
                load(k0_u[:, half].bitcast(mybir.dt.uint32),
                     k0.rearrange("(a k p) n -> a p k n", a=2, p=P)[half], k0_in)
            load(k2_u.bitcast(mybir.dt.uint32), by_rows(k2), k2_in)
            load(k1_u.bitcast(mybir.dt.uint32), by_rows(k1), k1_in)
            sp.wait_ge(s_done, NU)
            for r in range(4):
                for j in range(4):
                    sp.dma_start(
                        Kst[32 * r:32 * r + 32, j::4, :, :].rearrange("p m b n -> p m (b n)"),
                        KHL[32 * j:32 * j + 32, r // 2, :, :]).then_inc(k_stacked, 16)

            def stack_queries(a, g):
                wait_apart(sp, q_lo, nth(a, NG, g))
                wait_apart(sp, s_done, nth(a, NU, 4 * (g - 2) + 3))
                for r in range(4):
                    for j in range(4):
                        sp.dma_start(Qst[32 * r:32 * r + 32, g % 2, j, :],
                                     Qhl[32 * j:32 * j + 32, g % 2, r % 2, :])\
                          .then_inc(q_stacked[g % 2], 16)

            def keep_x1(a):
                wait_apart(sp, x1_ready, nth(a, NT, NT - 1))
                sp.dma_start(R_flat, X_flat).then_inc(r_copied, 16)

            def load_next(a):
                wait_apart(sp, xb_ready, nth(a, NT, NT - 1))
                sp.dma_start(Y_flat, x_v[a + 1]).then_inc(x_loaded, 16)

            def store(f):
                wait_apart(sp, out_ready, nth(f, NT, NT - 1))
                sp.dma_start(out_v[f], R_flat).then_inc(out_stored, 16)
                wait_apart(sp, out_stored, nth(f, 16, 15))

            load_next(0)
            keep_x1(0)
            for g in range(G):
                stack_queries(1, g)
            load_next(1)
            with sp.Fori(1, CHUNKS - 2) as i:
                store(i - 1)
                keep_x1(i)
                for g in range(G):
                    stack_queries(i + 1, g)
                load_next(i + 1)
            store(CHUNKS - 3)
            keep_x1(CHUNKS - 2)
            for g in range(G):
                stack_queries(CHUNKS - 1, g)
            store(CHUNKS - 2)
            keep_x1(CHUNKS - 1)
            for t in range(TT):
                sp.wait_ge(out_ready, nth(CHUNKS - 1, NT, t))
                sp.dma_start(out.rearrange("(c p t) d -> c p t d", p=P, t=TT)[CHUNKS - 1, :, t],
                             R[:, t, :]).then_inc(out_stored, 16)
            sp.wait_ge(out_stored, (CHUNKS - 1 + TT) * 16)

        @block.gpsimd
        def _(pool):
            pool.memset(ident[:, :], 0.0).then_inc(ident_zero, 1)
            pool.memset(Kst[:, :, :, :], 0.0).then_inc(k_zero, 1)
            pool.memset(minus_one[:, :], -1.0).then_inc(one_made, 1)
            pool.memset(halves[:, 0, :], -0.5).then_inc(half_made, 1)
            pool.memset(halves[:, 1, :], EPS).then_inc(half_made, 1)
            pool.memset(V[:, :, :, :], 1.0).then_inc(v_ones, 1)
            pool.wait_ge(ident_zero, 1)
            pool.affine_select(out=ident[:, :], in_=ident[:, :], compare_op=ALU.not_equal, fill=1.0,
                               base=0, pattern=[[-1, P]], channel_multiplier=1).then_inc(ident_made, 1)

            def attend(item, a, first):
                kind, n = item
                if kind in ("LN", "WO"):
                    r, w = (0, slice(0, TT)) if kind == "LN" else (1 + n, slice(n, n + 1))
                    pool.wait_ge(mv_ready, nth(a, NR, r))
                    pool.tensor_tensor(var_eps[:, w], mv[:, w, 1], halves[:, 1, w], ALU.add)\
                        .then_inc(var_ready, 1)
                    pool.wait_ge(var_ready, nth(a, NR, r))
                    pool.tensor_tensor(rstd[:, w], var_eps[:, w], halves[:, 0, w], ALU.pow)\
                        .then_inc(rstd_ready, 1)
                if kind == "CT":
                    if n == 0 and first:
                        pool.wait_ge(w0_made, KT)
                        pool.wait_ge(const_step, 5)
                    if n == 0 and not first:
                        pool.wait_ge(r_copied, nth(a - 1, 16, 15))
                        pool.wait_ge(xn_ready, nth(a - 1, NX, NX - 1))
                    if n == 0:
                        pool.wait_ge(x_loaded, nth(a, 16, 15))
                    pool.tensor_tensor(X[:, n, :], Y[:, n, :], bo_b[:, :], ALU.add).then_inc(xb_ready, 1)
                if kind == "PV":
                    g, t = divmod(n, TT)
                    pool.wait_ge(pv_scaled, nth(a, NU, n))
                    pool.tensor_tensor(
                        attn[:, t, g * P:(g + 1) * P].rearrange("p (j d) -> p j d", j=4),
                        pvs[:, n % 2, :, 0:HEAD], pvs[:, n % 2, :, HEAD:2 * HEAD], ALU.add)\
                        .then_inc(attn_ready, 1)

            pool.wait_ge(half_made, 2)
            for item in FIRST_ITEMS:
                attend(item, 0, True)
            for item in LOOP_ITEMS:
                attend(item, 1, False)
            for _, f0, f1 in LOOPS:
                with pool.Fori(f0, f1) as i:
                    for item in LOOP_ITEMS:
                        attend(item, i + 1, False)

        @block.scalar
        def _(act):
            for m in range(KT):
                act.wait_ge(k_float, m + 1)
                nc.scalar.activation(KHL[:, 0, m, :], Kf[m % 2], ACT.Copy).then_inc(k_hi, 1)
            act.wait_ge(wq_in, 16)
            nc.scalar.activation(Wq_hi[:, :, :], Wq_f, ACT.Copy, scale=WS).then_inc(w_hi, 1)

            def attend(item, a, first=False, second=False):
                kind, n = item
                if kind in ("T1", "T2"):
                    k = n + (TT if kind == "T2" else 0)
                    bank = (FIRST_BANK if first else LOOP_BANK)[item]
                    dst = xT_hi if kind == "T1" else hT_hi
                    act.wait_ge(xn_turned, nth(a, NX, k))
                    nc.scalar.activation(dst[:, :, n * P:(n + 1) * P],
                                         banks[bank][:, :].rearrange("p (k n) -> p k n", k=KT),
                                         ACT.Copy, scale=XS if kind == "T1" else h_scale)\
                        .then_inc(xt_hi, 1)
                if kind == "Q":
                    bank = banks[(FIRST_BANK if first else LOOP_BANK)[item]]
                    act.wait_ge(q_done, nth(a, NG, n))
                    if first and n == 0:
                        act.wait_ge(bq_in, 16)
                    if first and n >= 2:
                        act.wait_ge(s_done, 4 * (n - 2) + 4)
                    if second and n < 2:
                        act.wait_ge(s_done, 4 * (n + 2) + 4)
                    if not first and not (second and n < 2):
                        act.wait_ge(q_stacked[n % 2], ((a - 1) * STACK_USES + n // 2) * STACKS)
                    nc.scalar.activation(Qhl[:, n % 2, 0, :], bank[:, :], ACT.Identity,
                                         bias=bq_c[:, n:n + 1], scale=1 / (XS * WS))
                    if not (first and n == 0):
                        act.wait_ge(q_lo, nth(a, NG, n - 1))
                    nc.scalar.activation(Qf[:, :], bank[:, :], ACT.Identity, bias=bq_c[:, n:n + 1],
                                         scale=1 / (XS * WS)).then_inc(q_split, 1)
                if kind == "S":
                    bank = banks[(FIRST_BANK if first else LOOP_BANK)[item]]
                    act.wait_ge(s_max, nth(a, NU, n))
                    for j in range(4):
                        last = nc.scalar.activation(
                            Pf[:, n % 2, j * P:(j + 1) * P], bank[:, j * P:(j + 1) * P], ACT.Exp,
                            bias=nmax[:, n % 2, j:j + 1], scale=1.0)
                    last.then_inc(p_ready, 1)
                if kind == "T":
                    bank = banks[(FIRST_BANK if first else LOOP_BANK)[item]]
                    act.wait_ge(p_turned, nth(a, NU, n))
                    nc.scalar.activation(PT_hi[:, n % 2, :], bank[:, :], ACT.Copy, scale=PS)\
                        .then_inc(pt_hi, 1)
                if kind == "CT":
                    bank = banks[(FIRST_BANK if first else LOOP_BANK)[item]]
                    act.wait_ge(c_turned, nth(a, NT, n))
                    nc.scalar.activation(cT_hi[:, n % 2, :], bank[:, :], ACT.Copy).then_inc(ct_hi, 1)

            def feed(slot, f):
                kind, n, q = slot
                if kind == "L0" or (kind == "L1" and q == 3):
                    e = n + (FT if kind == "L1" else 0)
                    dst = h0_hi[:, n, :] if kind == "L0" else h1_hi[:, n % 2, :]
                    act.wait_ge(ffn_done, nth(f, NF, e))
                    nc.scalar.activation(dst, banks[e % 2][:, :], ACT.Relu).then_inc(ffn_hi, 1)

            for item in FIRST_ITEMS:
                if item == ("Q", 1):
                    for b in range(BATCHES):
                        act.wait_ge(v_float, b + 1)
                        act.wait_ge(v_ones, 1)
                        nc.scalar.activation(V[:, b, :, 0:HEAD],
                                             Vf[b].rearrange("p (h d) -> p h d", h=HEADS),
                                             ACT.Copy, scale=VS).then_inc(v_hi, 1)
                if item == ("S", 1):
                    act.wait_ge(scalars_in, 5 * 16)
                    nc.scalar.activation(c[:, 0:2], scal[:, 0:2], ACT.Tanh).then_inc(const_tanh, 1)
                if item == ("S", 3):
                    act.wait_ge(wo_in, 16)
                    nc.scalar.activation(Wo_hi[:, :, :], Wo_f, ACT.Copy, scale=WS).then_inc(w_hi, 1)
                if item[0] == "PV" and item[1] % 4 == 3:
                    q = slice(item[1] - 3, item[1] + 1)
                    if item[1] == 3:
                        act.wait_ge(k2_in, 16)
                        act.wait_ge(one_made, 1)
                    nc.scalar.activation(W2[:, q, :], k2_u[:, q, :], ACT.Identity, bias=minus_one[:, :],
                                         scale=2.0, saturate=False).then_inc(w2_made, 1)
                if item == ("T2", 0):
                    act.wait_ge(w2_made, 4)
                attend(item, 0, first=True)
            act.wait_ge(k1_in, 16)
            act.wait_ge(w_lo, 2)
            act.wait_ge(v_done, BATCHES)
            for s, slot in enumerate(SLOTS):
                if slot[0] == "L0" and slot[1] % 2 == 0:
                    k = slot[1] // 2
                    nc.scalar.activation(W1[:, k, :], k1_u[:, k, :], ACT.Identity, bias=w1_b,
                                         scale=w1_a, saturate=False).then_inc(w1_made[0], 1)
                    act.wait_ge(w1_made[0], k + 1)
                feed(slot, 0)
                for item in WEAVE.get(s, ()):
                    attend(item, 1, second=True)
            for _, f0, f1 in LOOPS:
                with act.Fori(f0, f1) as i:
                    for s, slot in enumerate(SLOTS):
                        feed(slot, i)
                        for item in WEAVE.get(s, ()):
                            attend(item, i + 1)
            for slot in SLOTS:
                feed(slot, CHUNKS - 1)

        @block.vector
        def _(dve):
            V_ = nc.vector
            for b in range(BATCHES):
                dve.wait_ge(ctx_turned, b + 1)
                V_.tensor_copy(ctxT[:, :, b * P:(b + 1) * P],
                               banks[6 + b][:, :].rearrange("p (k n) -> p k n", k=KT))\
                    .then_inc(ctx_taken, 1)
            dve.wait_ge(bk_in, 16)
            for m in range(KT):
                dve.wait_ge(k_done, m + 1)
                if m >= 2:
                    dve.wait_ge(k_lo, m - 1)
                V_.tensor_scalar(Kf[m % 2], banks[m][:, 0:BATCHES * P], bk_c[:, m:m + 1], SCALE,
                                 ALU.add, ALU.mult).then_inc(k_float, 1)
                dve.wait_ge(k_hi, m + 1)
                V_.tensor_tensor(KHL[:, 1, m, :], Kf[m % 2], KHL[:, 0, m, :], ALU.subtract).then_inc(k_lo, 1)

            dve.wait_ge(k_zero, 1)
            dve.wait_ge(k_lo, KT)
            for j in range(4):
                rows = slice(HEAD * j, HEAD * j + HEAD)
                V_.tensor_copy(Kst[rows, j::4, :, :], KHL[rows, :, :, 0:P].rearrange("p a m n -> p m a n"))\
                    .then_inc(k_spread, 1)

            def follow_scalars():
                dve.wait_ge(scalars_in, 5 * 16)
                V_.tensor_scalar(c[:, 2:4], scal[:, 2:4], 0.0, None, ALU.is_ge).then_inc(const_step, 1)
                dve.wait_ge(const_step, 1)
                V_.tensor_scalar(c[:, 4:6], c[:, 2:4], 2.0, -1.0, ALU.mult, ALU.add).then_inc(const_step, 1)
                dve.wait_ge(const_step, 2)
                dve.wait_ge(const_tanh, 1)
                V_.tensor_scalar(h_scale, sgn0, XS, None, ALU.mult)
                V_.tensor_scalar(w1_a, sgn1, 2 * W1S, None, ALU.mult)
                V_.tensor_scalar(w1_b, sgn1, -W1S, None, ALU.mult)
                V_.tensor_scalar(wo_scale, tanh_x, 1 / (VS * WS), None, ALU.mult)
                V_.tensor_scalar(fin_part, tanh_f, scal[:, 4:5], OUTS, ALU.mult, ALU.mult)
                V_.tensor_tensor(c[:, 11:13], scal[:, 2:4], c[:, 4:6], ALU.mult).then_inc(const_step, 1)
                dve.wait_ge(const_step, 3)
                V_.tensor_scalar(fin, fin_part, abs0, abs1, ALU.mult, ALU.mult)\
                    .then_inc(const_step, 1)
                dve.wait_ge(bo_in, 16)
                V_.tensor_scalar(bo_b[:, :], bo_b[:, :], tanh_x, None, ALU.mult).then_inc(const_step, 1)

            def make_w0(k):
                V_.tensor_tensor(W0[:, k, :], k0_u[:, 0, k, :], k0_u[:, 1, k, :], ALU.subtract,
                                 saturate=False).then_inc(w0_made, 1)

            def normalise(a, k, src, t, first):
                if not (first and k < 2):
                    dve.wait_ge(xn_turned, nth(a, NX, k - 2))
                V_.tensor_scalar(xn[:, k % 2, :], src, mv[:, t, 0:1], rstd[:, t:t + 1],
                                 ALU.subtract, ALU.mult).then_inc(xn_ready, 1)

            def attend(item, a, first):
                kind, n = item
                bank = banks[(FIRST_BANK if first else LOOP_BANK)[item]] if kind in ON_PE else None
                if kind == "LN":
                    dve.wait_ge(x_loaded, nth(a, 16, 15))
                    for t in range(TT):
                        V_.bn_stats(stats[:, t, :], Y[:, t, :]).then_inc(ln_step, 1)
                    wait_apart(dve, ln_step, nth(a, NLN, TT - 1))
                    for t in range(TT):
                        last = V_.bn_aggr(mv[:, t, :], stats[:, t, :])
                    last.then_inc(mv_ready, 1)
                if kind == "N1":
                    if n == 0:
                        dve.wait_ge(rstd_ready, nth(a, NR, 0))
                    normalise(a, n, Y[:, n, :], n, first)
                if kind in ("T1", "T2"):
                    k = n + (TT if kind == "T2" else 0)
                    hi, lo = (xT_hi, xT_lo) if kind == "T1" else (hT_hi, hT_lo)
                    dve.wait_ge(xt_hi, nth(a, NX, k))
                    V_.scalar_tensor_tensor(
                        out=lo[:, :, n * P:(n + 1) * P],
                        in0=bank[:, :].rearrange("p (k n) -> p k n", k=KT),
                        scalar=XS if kind == "T1" else h_scale, in1=hi[:, :, n * P:(n + 1) * P],
                        op0=ALU.mult, op1=ALU.subtract).then_inc(xt_lo, 1)
                if kind == "Q":
                    dve.wait_ge(q_split, nth(a, NG, n))
                    V_.tensor_tensor(Qhl[:, n % 2, 1, :], Qf[:, :], Qhl[:, n % 2, 0, :], ALU.subtract)\
                        .then_inc(q_lo, 1)
                if kind == "S":
                    dve.wait_ge(s_done, nth(a, NU, n))
                    V_.tensor_reduce(nmax[:, n % 2, :], bank[:, :].rearrange("p (j k) -> p j k", j=4),
                                     AX.X, ALU.max, negate=True).then_inc(s_max, 1)
                if kind == "T":
                    dve.wait_ge(pt_hi, nth(a, NU, n))
                    V_.scalar_tensor_tensor(out=PT_lo[:, n % 2, :], in0=bank[:, :], scalar=PS,
                                            in1=PT_hi[:, n % 2, :], op0=ALU.mult, op1=ALU.subtract)\
                        .then_inc(pt_lo, 1)
                if kind == "PV":
                    v = bank[:, :].rearrange("p (j n) -> p j n", j=4)
                    dve.wait_ge(pv_done, nth(a, NU, n))
                    if not (first and n < 2):
                        dve.wait_ge(attn_ready, nth(a, NU, n - 2))
                    V_.reciprocal(rden[:, n % 2, :], v[:, :, 2 * HEAD]).then_inc(recip_done, 1)
                    dve.wait_ge(recip_done, nth(a, NU, n))
                    V_.tensor_tensor(
                        pvs[:, n % 2, :, :], v[:, :, 0:2 * HEAD],
                        rden[:, n % 2, :].rearrange("p (j o) -> p j o", o=1).to_broadcast([P, 4, 2 * HEAD]),
                        ALU.mult).then_inc(pv_scaled, 1)
                if kind == "CT":
                    dve.wait_ge(ct_hi, nth(a, NT, n))
                    V_.tensor_tensor(cT_lo[:, n % 2, :], bank[:, :], cT_hi[:, n % 2, :], ALU.subtract)\
                        .then_inc(ct_lo, 1)
                if kind == "WO":
                    dve.wait_ge(wo_done, nth(a, NT, n))
                    dve.wait_ge(xb_ready, nth(a, NT, n))
                    V_.scalar_tensor_tensor(out=X[:, n, :], in0=bank[:, :], scalar=wo_scale,
                                            in1=X[:, n, :], op0=ALU.mult, op1=ALU.add)\
                        .then_inc(x1_ready, 1)
                    dve.wait_ge(x1_ready, nth(a, NT, n))
                    V_.bn_stats(stats[:, n, :], X[:, n, :]).then_inc(ln_step, 1)
                    wait_apart(dve, ln_step, nth(a, NLN, TT + n))
                    V_.bn_aggr(mv[:, n, :], stats[:, n, :]).then_inc(mv_ready, 1)
                if kind == "N2":
                    dve.wait_ge(rstd_ready, nth(a, NR, 1 + n))
                    normalise(a, TT + n, X[:, n, :], n, first)

            def feed(slot, f):
                kind, n, q = slot
                if kind == "L0" or (kind == "L1" and q == 3):
                    e = n + (FT if kind == "L1" else 0)
                    hi, lo = (h0_hi[:, n, :], h0_lo[:, n, :]) if kind == "L0" else (
                        h1_hi[:, n % 2, :], h1_lo[:, n % 2, :])
                    dve.wait_ge(ffn_hi, nth(f, NF, e))
                    V_.scalar_tensor_tensor(out=lo, in0=banks[e % 2][:, :], scalar=0.0, in1=hi,
                                            op0=ALU.max, op1=ALU.subtract).then_inc(ffn_lo, 1)
                if kind == "L2" and n == FT - 1:
                    dve.wait_ge(r_copied, nth(f, 16, 15))
                    for t in range(TT):
                        dve.wait_ge(l2_done, nth(f, NT, t))
                        V_.scalar_tensor_tensor(out=R[:, t, :], in0=banks[2 + t][:, :], scalar=fin,
                                                in1=R[:, t, :], op0=ALU.mult, op1=ALU.add)\
                            .then_inc(out_ready, 1)

            for item in FIRST_ITEMS:
                if item == ("Q", 0):
                    dve.wait_ge(w_hi, 1)
                    V_.scalar_tensor_tensor(out=Wq_lo[:, :, :].rearrange("p k n -> p (k n)"),
                                            in0=Wq_f.rearrange("p k n -> p (k n)"), scalar=WS,
                                            in1=Wq_hi[:, :, :].rearrange("p k n -> p (k n)"),
                                            op0=ALU.mult, op1=ALU.subtract).then_inc(w_lo, 1)
                if item == ("Q", 1):
                    dve.wait_ge(bv_in, 16)
                    for b in range(BATCHES):
                        dve.wait_ge(v_done, b + 1)
                        V_.tensor_tensor(Vf[b], banks[4 + b][:, :], bv_b[:, :], ALU.add)\
                            .then_inc(v_float, 1)
                        dve.wait_ge(v_hi, b + 1)
                        V_.scalar_tensor_tensor(
                            out=V[:, b, :, HEAD:2 * HEAD], in0=Vf[b].rearrange("p (h d) -> p h d", h=HEADS),
                            scalar=VS, in1=V[:, b, :, 0:HEAD], op0=ALU.mult, op1=ALU.subtract)\
                            .then_inc(v_lo, 1)
                if item == ("S", 3):
                    follow_scalars()
                    dve.wait_ge(w_hi, 2)
                    V_.scalar_tensor_tensor(out=Wo_lo[:, :, :].rearrange("p k n -> p (k n)"),
                                            in0=Wo_f.rearrange("p k n -> p (k n)"), scalar=WS,
                                            in1=Wo_hi[:, :, :].rearrange("p k n -> p (k n)"),
                                            op0=ALU.mult, op1=ALU.subtract).then_inc(w_lo, 1)
                if item == ("S", 4):
                    dve.wait_ge(k0_in, 32)
                if item[0] == "S" and item[1] in (4, 7, 10, 13):
                    make_w0(item[1] // 3 - 1)
                if item == ("T2", 0):
                    dve.wait_ge(w2_made, 4)
                attend(item, 0, True)
            dve.wait_ge(k1_in, 16)
            for s, slot in enumerate(SLOTS):
                if slot[0] == "L0" and slot[1] % 2 == 0:
                    k = FT // 2 + slot[1] // 2
                    V_.tensor_scalar(W1[:, k, :], k1_u[:, k, :], w1_a, w1_b, ALU.mult, ALU.add,
                                     saturate=False).then_inc(w1_made[1], 1)
                    dve.wait_ge(w1_made[1], slot[1] // 2 + 1)
                feed(slot, 0)
                for item in WEAVE.get(s, ()):
                    attend(item, 1, False)
            for _, f0, f1 in LOOPS:
                with dve.Fori(f0, f1) as i:
                    for s, slot in enumerate(SLOTS):
                        feed(slot, i)
                        for item in WEAVE.get(s, ()):
                            attend(item, i + 1, False)
            for slot in SLOTS:
                feed(slot, CHUNKS - 1)

        @block.tensor
        def _(pe):
            mm, turn = nc.tensor.matmul, nc.tensor.transpose
            pe.wait_ge(ident_made, 1)
            pe.wait_ge(ctx_in, 16)
            for b in range(BATCHES):
                for k in range(KT):
                    last = turn(banks[6 + b][:, k * P:(k + 1) * P], ctx_f[:, b, k * P:(k + 1) * P],
                                ident[:, :])
                last.then_inc(ctx_turned, 1)
            pe.wait_ge(ctx_taken, BATCHES)
            pe.wait_ge(wk_in, 16)
            for m in range(KT):
                for k in range(KT):
                    last = mm(banks[m][:, 0:BATCHES * P], Wk_f[:, k, m * P:(m + 1) * P], ctxT[:, k, :],
                              start=k == 0, stop=k == KT - 1)
                last.then_inc(k_done, 1)
            def make_values():
                pe.wait_ge(wv_in, 16)
                for b in range(BATCHES):
                    for k in range(KT):
                        last = mm(banks[4 + b][:, :], ctxT[:, k, b * P:(b + 1) * P], Wv_f[:, k, :],
                                  start=k == 0, stop=k == KT - 1)
                    last.then_inc(v_done, 1)

            def released(item, a):
                kind, n = item
                return {"T1": (xt_lo, NX, n), "T2": (xt_lo, NX, TT + n), "Q": (q_split, NG, n),
                        "S": (p_ready, NU, n), "T": (pt_lo, NU, n), "PV": (pv_scaled, NU, n),
                        "CT": (ct_lo, NT, n), "WO": (x1_ready, NT, n)}[kind]

            def attend(item, a, batch, first):
                kind, n = item
                if kind not in ON_PE:
                    return
                if first:
                    bank, before, since = FIRST_BANK[item], user_before(FIRST_ITEMS, FIRST_BANK, item), a
                else:
                    bank, before, since = LOOP_BANK[item], user_before(LOOP_ITEMS, LOOP_BANK, item), a
                    if before is None:
                        before, since = [i for i in LOOP_ITEMS if LOOP_BANK.get(i) == bank][-1], a - 1
                if before is not None:
                    signal, per_chunk, m = released(before, a)
                    pe.wait_ge(signal, nth(since, per_chunk, m))
                bank = banks[bank]
                if kind in ("T1", "T2"):
                    k = n + (TT if kind == "T2" else 0)
                    pe.wait_ge(xn_ready, nth(a, NX, k))
                    for d in range(KT):
                        last = turn(bank[:, d * P:(d + 1) * P], xn[:, k % 2, d * P:(d + 1) * P],
                                    ident[:, :])
                    last.then_inc(xn_turned, 1)
                if kind == "Q":
                    if n == 0:
                        pe.wait_ge(xt_lo, nth(a, NX, TT - 1))
                    for k in range(KT):
                        w_h, w_l = (w[:, k, n * P:(n + 1) * P] for w in (Wq_hi, Wq_lo))
                        mm(bank[:, :], w_h, xT_hi[:, k, :], start=k == 0, stop=False)
                        mm(bank[:, :], w_h, xT_lo[:, k, :], start=False, stop=False)
                        last = mm(bank[:, :], w_l, xT_hi[:, k, :], start=False, stop=k == KT - 1)
                    last.then_inc(q_done, 1)
                if kind == "S":
                    g, t = divmod(n, TT)
                    if first:
                        if t == 0:
                            pe.wait_ge(q_lo, g + 1)
                        for part in range(4):
                            last = mm(bank[:, :], Qhl[:, g % 2, part % 2, t * P:(t + 1) * P],
                                      Kst[:, 4 * g:4 * g + 4, part // 2, :],
                                      start=part == 0, stop=part == 3)
                        last.then_inc(s_done, 1)
                        return
                    if t == 0:
                        pe.wait_ge(q_stacked[g % 2], ((a - 1) * STACK_USES + g // 2 + 1) * STACKS)
                    for j in range(4):
                        last = mm(bank[:, j * P:(j + 1) * P], Qst[:, g % 2, j, t * P:(t + 1) * P],
                                  Kst[:, 4 * g + j, batch, :], start=True, stop=True)
                    last.then_inc(s_done, 1)
                if kind == "T":
                    pe.wait_ge(p_ready, nth(a, NU, n))
                    for j in range(4):
                        last = turn(bank[:, j * P:(j + 1) * P], Pf[:, n % 2, j * P:(j + 1) * P],
                                    ident[:, :])
                    last.then_inc(p_turned, 1)
                if kind == "PV":
                    g, t = divmod(n, TT)
                    pe.wait_ge(pt_lo, nth(a, NU, n))
                    for j in range(4):
                        o, v = bank[:, j * P:j * P + VW - 1], V[:, batch, 4 * g + j, 0:VW - 1]
                        mm(o, PT_hi[:, n % 2, j * P:(j + 1) * P], v, start=True, stop=False)
                        last = mm(o, PT_lo[:, n % 2, j * P:(j + 1) * P], v, start=False, stop=True)
                    last.then_inc(pv_done, 1)
                if kind == "CT":
                    pe.wait_ge(attn_ready, nth(a, NU, (G - 1) * TT + n))
                    for k in range(KT):
                        last = turn(bank[:, k * P:(k + 1) * P], attn[:, n, k * P:(k + 1) * P],
                                    ident[:, :])
                    last.then_inc(c_turned, 1)
                if kind == "WO":
                    pe.wait_ge(ct_lo, nth(a, NT, n))
                    for k in range(KT):
                        c_h, c_l = (w[:, n % 2, k * P:(k + 1) * P] for w in (cT_hi, cT_lo))
                        mm(bank[:, :], c_h, Wo_hi[:, k, :], start=k == 0, stop=False)
                        mm(bank[:, :], c_h, Wo_lo[:, k, :], start=False, stop=False)
                        last = mm(bank[:, :], c_l, Wo_hi[:, k, :], start=False, stop=k == KT - 1)
                    last.then_inc(wo_done, 1)

            def feed(slot, f):
                kind, n, q = slot
                if kind == "L0":
                    if n == 0:
                        wait_apart(pe, xt_lo, nth(f, NX, NX - 1))
                    if n >= 2:
                        wait_apart(pe, ffn_lo, nth(f, NF, n - 2))
                    for k in range(KT):
                        w = W0[:, k, n * P:(n + 1) * P]
                        mm(banks[n % 2][:, :], w, hT_hi[:, k, :], start=k == 0, stop=False)
                        last = mm(banks[n % 2][:, :], w, hT_lo[:, k, :], start=False, stop=k == KT - 1)
                    last.then_inc(ffn_done, 1)
                if kind == "L1":
                    if q == 0:
                        wait_apart(pe, ffn_lo, nth(f, NF, FT + n - 2))
                    if n == 0:
                        wait_apart(pe, ffn_lo, nth(f, NF, 4 * q + 3))
                    for k in range(4 * q, 4 * q + 4):
                        w = W1[:, k, n * P:(n + 1) * P]
                        mm(banks[n % 2][:, :], w, h0_hi[:, k, :], start=k == 0, stop=False)
                        last = mm(banks[n % 2][:, :], w, h0_lo[:, k, :], start=False, stop=k == FT - 1)
                    if q == 3:
                        last.then_inc(ffn_done, 1)
                if kind == "L2":
                    wait_apart(pe, ffn_lo, nth(f, NF, FT + n))
                    for t in range(TT):
                        tok = slice(t * P, (t + 1) * P)
                        mm(banks[2 + t][:, :], h1_hi[:, n % 2, tok], W2[:, n, :],
                           start=n == 0, stop=False)
                        last = mm(banks[2 + t][:, :], h1_lo[:, n % 2, tok], W2[:, n, :],
                                  start=False, stop=n == FT - 1)
                        if n == FT - 1:
                            last.then_inc(l2_done, 1)

            for item in FIRST_ITEMS:
                if item == ("Q", 0):
                    pe.wait_ge(w_lo, 1)
                    pe.wait_ge(k_lo, KT)
                if item == ("Q", 1):
                    make_values()
                if item == ("S", 0):
                    pe.wait_ge(k_spread, 4)
                if item == ("PV", 0):
                    pe.wait_ge(v_lo, BATCHES)
                if item == ("WO", 0):
                    pe.wait_ge(w_lo, 2)
                attend(item, 0, 0, True)
            pe.wait_ge(k_stacked, 16 * 16)
            pe.wait_ge(w0_made, KT)
            pe.wait_ge(w2_made, 4)
            for s, slot in enumerate(SLOTS):
                if slot[:2] == ("L1", 0):
                    pe.wait_ge(w1_made[slot[2] // 2], 4 * (slot[2] % 2) + 4)
                feed(slot, 0)
                for item in WEAVE.get(s, ()):
                    attend(item, 1, 0, False)
            for batch, f0, f1 in LOOPS:
                with pe.Fori(f0, f1) as i:
                    for s, slot in enumerate(SLOTS):
                        feed(slot, i)
                        for item in WEAVE.get(s, ()):
                            attend(item, i + 1, batch, False)
            for slot in SLOTS:
                feed(slot, CHUNKS - 1)


_INS = ["x", "ctx_1024", "g_xattn", "g_ffn", "L0_xattn_Wq", "L0_xattn_Wk", "L0_xattn_Wv", "L0_xattn_Wo",
        "L0_xattn_bq", "L0_xattn_bk", "L0_xattn_bv", "L0_xattn_bo", "L0_ffn_k0", "L0_ffn_k1",
        "L0_ffn_k2", "L0_ffn_s0", "L0_ffn_s1", "L0_ffn_s2"]


def kernel(**inputs):
    import numpy as _np
    import concourse.bacc as _bacc
    from concourse import mybir as _mybir
    from concourse.bass_utils import run_bass_kernel_spmd as _run

    nc = _bacc.Bacc("TRN2", target_bir_lowering=False, num_devices=1)
    arrays, args = {}, []
    for name in _INS:
        a = _np.ascontiguousarray(inputs[name])
        if a.ndim == 3:
            a = a.reshape(-1, a.shape[-1])
        if a.ndim == 0:
            a = a.reshape(1)
        if a.dtype == _np.bool_:
            a = a.view(_np.uint32)
        arrays[f"in_{name}_dram"] = a
        args.append(nc.dram_tensor(f"in_{name}_dram", a.shape, _mybir.dt.from_np(a.dtype),
                                   kind="ExternalInput").ap())
    shape = inputs["x"].shape
    out = nc.dram_tensor("out_dram", (shape[0] * shape[1], shape[2]), _mybir.dt.float32,
                         kind="ExternalOutput").ap()
    gated_block_kernel(nc, *args, out)
    r = _run(nc, [arrays], core_ids=[0])
    return r.results[0]["out_dram"].reshape(shape)
```

```python
from contextlib import ExitStack

import concourse.bass as bass
from concourse import mybir

P = 128


def gated_block_kernel(nc: bass.Bass, x, ctx, g_xattn, g_ffn, Wq, Wk, Wv, Wo, bq, bk, bv, bo,
                       k0, k1, k2, s0, s1, s2, out):
    f32, f16, f8 = mybir.dt.float32, mybir.dt.float16, mybir.dt.float8e5
    u8, u32 = mybir.dt.uint8, mybir.dt.uint32
    ALU = mybir.AluOpType
    ACT = mybir.ActivationFunctionType
    AX = mybir.AxisListType

    TOKENS, D = x.shape
    KEYS_ALL = ctx.shape[0]
    BATCHES = KEYS_ALL // P
    F = k1.shape[0]
    HEAD = 32
    HEADS = D // HEAD
    KT = D // P
    FT = F // P
    G = HEADS // 4
    CHUNK = 512
    TT = CHUNK // P
    CHUNKS = TOKENS // CHUNK
    PER_BATCH = CHUNKS // BATCHES
    U = G * TT
    VW = 2 * HEAD + 2
    EPS = 1e-5
    XS = 64.0
    WS = 256.0
    VS = 16.0
    PS = 1024.0
    W1S = 2.0 ** -11
    OUTS = 4.0 / (XS / 2 * W1S)
    SCALE = HEAD ** -0.5

    SLOTS = [("L0", n, 0) for n in range(FT)]
    for n in range(FT):
        SLOTS += [("L1", n, 0), ("L1", n, 1)] + ([("L2", n - 1, 0)] if 0 < n < FT - 1 else [])
        SLOTS += [("L1", n, 2), ("L1", n, 3)]
    SLOTS += [("L2", FT - 2, 0), ("L2", FT - 1, 0)]
    WEAVE = {}

    def weave(slot, *item):
        WEAVE.setdefault(slot, []).append(item)

    FIRST_UNIT = 17
    for t in range(TT):
        weave(t, "LN", t)
    weave(4, "N1", 0)
    weave(5, "N1", 1)
    for t in range(TT):
        weave(6 + t, "T1", t)
        if t + 2 < TT:
            weave(6 + t, "N1", t + 2)
    for g, slot in enumerate((10, 12, FIRST_UNIT + 17, FIRST_UNIT + 33)):
        weave(slot, "Q", g)
    for u in range(U):
        weave(FIRST_UNIT + 4 * u + 2, "T", u)
        weave(FIRST_UNIT + 4 * u + 4, "PV", u)
    for u in range(U):
        weave(FIRST_UNIT + 4 * u, "S", u)
    for t in range(TT):
        weave(FIRST_UNIT + 55 + 4 * t, "CT", t)
        weave(FIRST_UNIT + 57 + 4 * t, "WO", t)
        weave(FIRST_UNIT + 58 + 4 * t, "N2", t)
        weave(FIRST_UNIT + 61 + 4 * t, "T2", t)
    LOOP_ITEMS = [item for slot in sorted(WEAVE) for item in WEAVE[slot]]

    def first_items(turn_first):
        items = [("K", 0)] + [("LN", t) for t in range(TT)]
        items += [("K", 1), ("N1", 0), ("N1", 1), ("CUT_Q", 0), ("K", 2), ("CUT_Q", 1), ("K", 3)]
        items += [("T1", 0), ("N1", 2), ("CUT_Q", 2), ("T1", 1), ("N1", 3), ("T1", 2), ("CUT_Q", 3), ("T1", 3)]
        items += [("SPREAD", 0), ("Q", 0), ("V", 0)]
        scores_turn = [("T", U, 2), ("S", U, 0)] if turn_first else [("S", U, 0), ("T", U, 2)]
        for k in range(U + 8):
            for kind, count, behind in scores_turn + [
                    ("PV", U, 3), ("CT", TT, U), ("WO", TT, U + 1), ("N2", TT, U + 2), ("T2", TT, U + 3),
                    ("CUT_O", KT, 4), ("W0", KT, 8), ("W1", W1_EARLY, U - 1)]:
                items += [(kind, k - behind)] if 0 <= k - behind < count else []
            items += {1: [("Q", 1)], 2: [("V", 1)], 3: [("SCALARS", 0)], 5: [("Q", 2)], 9: [("Q", 3)],
                      14: [("W2", 0)]}.get(k, [])
        return items

    W1_EARLY = 5
    LATE_WEIGHTS = {1: ("W0", KT), 3: ("W0", KT + 1), 5: ("W0", KT + 2), 6: ("W0", KT + 3),
                    7: ("W1", W1_EARLY), 8: ("W1", W1_EARLY + 1), 9: ("W1", W1_EARLY + 2)}
    FIRST_ITEMS = first_items(False)
    ACT_FIRST_ITEMS = first_items(True)
    LOOPS = ((0, 1, PER_BATCH - 1), (1, PER_BATCH - 1, CHUNKS - 1))
    ON_PE = ("T1", "Q", "S", "T", "PV", "CT", "WO", "T2")

    LOOP_BANK = {item: 6 + n % 2 for n, item in enumerate(i for i in LOOP_ITEMS if i[0] in ON_PE)}
    KIND_BANKS = {"T1": (6, 7), "Q": (0, 1), "S": (2, 3), "T": (6, 7), "PV": (4, 5),
                  "CT": (0, 1), "WO": (2, 3), "T2": (6, 7)}
    FIRST_BANK = {item: KIND_BANKS[item[0]][item[1] % 2] for item in FIRST_ITEMS if item[0] in ON_PE}

    def user_before(items, bank, item):
        before = [i for i in items[:items.index(item)] if bank.get(i) == bank[item]]
        return before[-1] if before else None

    es = ExitStack()
    with es:
        def sb(name, shape, dt):
            return es.enter_context(nc.sbuf_tensor(name, shape, dt))

        def sem(name):
            return es.enter_context(nc.semaphore(name))

        W0 = sb("W0", [P, KT, F], f8)
        W1 = sb("W1", [P, FT, F], f8)
        W2 = sb("W2", [P, FT, D], f8)
        Wq_hi, Wq_lo = sb("Wq_hi", [P, KT, D], f16), sb("Wq_lo", [P, KT, D], f16)
        Wo_hi, Wo_lo = sb("Wo_hi", [P, KT, D], f16), sb("Wo_lo", [P, KT, D], f16)
        Kst = sb("Kst", [P, HEADS, BATCHES, P], f16)
        V = sb("V", [P, BATCHES, HEADS, VW], f16)
        ident = sb("ident", [P, P], f32)
        scal = sb("scal", [P, 5], f32)
        c = sb("c", [P, 16], f32)
        bq_c, bk_c = sb("bq_c", [P, KT], f32), sb("bk_c", [P, KT], f32)
        bv_b = sb("bv_b", [P, D], f32)
        bo_b = sb("bo_b", [P, D], f32)

        Y = sb("Y", [P, TT, D], f32)
        XR = sb("XR", [P, 2, TT, D], f32)
        X, R = XR[:, 0], XR[:, 1]
        xn = sb("xn", [P, 2, D], f32)
        xT_hi, xT_lo = sb("xT_hi", [P, KT, CHUNK], f16), sb("xT_lo", [P, KT, CHUNK], f16)
        hT = sb("hT", [P, 2, KT, CHUNK], f16)
        hT_hi, hT_lo = hT[:, 0], hT[:, 1]
        Qf = sb("Qf", [P, CHUNK], f32)
        Qhl = sb("Qhl", [P, 2, 2, CHUNK], f16)
        Qst = sb("Qst", [P, 2, 4, CHUNK], f16)
        Pf = sb("Pf", [P, 2, 4 * P], f32)
        PT_hi, PT_lo = sb("PT_hi", [P, 2, 4 * P], f16), sb("PT_lo", [P, 2, 4 * P], f16)
        pvs = sb("pvs", [P, 2, 4, 2 * HEAD], f32)
        attn = sb("attn", [P, TT, D], f32)
        cT_hi, cT_lo = sb("cT_hi", [P, 2, KT * P], f16), sb("cT_lo", [P, 2, KT * P], f16)
        H0 = sb("H0", [P, 2, FT, CHUNK], f16)
        h0_hi, h0_lo = H0[:, 0], H0[:, 1]
        h1_hi, h1_lo = sb("h1_hi", [P, 2, CHUNK], f16), sb("h1_lo", [P, 2, CHUNK], f16)
        stats = sb("stats", [P, TT, 6], f32)
        mv = sb("mv", [P, TT, 2], f32)
        rstd = sb("rstd", [P, TT], f32)
        var_eps = sb("var_eps", [P, TT], f32)
        ones_mask, eleventh_mask, w1_mask = (sb(n, [P, 1], u32) for n in (
            "ones_mask", "eleventh_mask", "w1_mask"))
        halves = sb("halves", [P, 2, TT], f32)
        nmax = sb("nmax", [P, 2, 4], f32)
        rden = sb("rden", [P, 2, 4], f32)

        w1f = W1[:, :, :].rearrange("p k n -> p (k n)").bitcast(f32)
        fw = [w1f[:, w * KT * D:(w + 1) * KT * D].rearrange("p (k n) -> p k n", k=KT) for w in range(4)]
        Wk_f, Wv_f, Wq_f, Wo_f = fw
        k0_u = [t.bitcast(u8).rearrange("p (a k n) -> p a k n", a=2, k=KT)
                for t in (XR[:, 1].rearrange("p t d -> p (t d)"),
                          Qst[:, :, :, :].rearrange("p r j n -> p (r j n)"))]
        k1_u = H0[:, :, :, :].rearrange("p a k n -> p (a k n)").bitcast(u8).rearrange(
            "p (k n) -> p k n", k=FT)
        k2_u = hT[:, :, :, :].rearrange("p a k n -> p (a k n)").bitcast(u8).rearrange(
            "p (k n) -> p k n", k=FT)
        attn_f = attn[:, :, :].rearrange("p t d -> p (t d)")
        ctx_f = attn_f[:, 0:BATCHES * D].rearrange("p (b d) -> p b d", b=BATCHES)
        ctxT = attn_f[:, BATCHES * D:2 * BATCHES * D].rearrange("p (k n) -> p k n", k=KT)
        Kf = [Pf[:, n, 0:BATCHES * P] for n in range(2)]
        KHL = sb("KHL", [P, 2, KT, BATCHES * P], f16)
        Vf = [pvs[:, :, :, :].rearrange("p a j n -> p (a j n)"),
              h1_hi[:, :, :].rearrange("p a n -> p (a n)").bitcast(f32)]

        banks = [es.enter_context(nc.psum_tensor(f"bank{n}", [P, 512], f32)) for n in range(8)]

        scalars_in, bq_in, bk_in, bv_in, bo_in, ctx_in, wk_in, wv_in, wq_in, wo_in = (sem(n) for n in (
            "scalars_in", "bq_in", "bk_in", "bv_in", "bo_in", "ctx_in", "wk_in", "wv_in", "wq_in", "wo_in"))
        k0_in, k1_in, k2_in = [sem("k0_in0"), sem("k0_in1")], sem("k1_in"), sem("k2_in")
        ident_made, ident_zero, v_ones, half_made, masks_made = (
            sem(n) for n in ("ident_made", "ident_zero", "v_ones", "half_made", "masks_made"))
        const_tanh, const_step = sem("const_tanh"), sem("const_step")
        ctx_turned, ctx_taken = sem("ctx_turned"), sem("ctx_taken")
        k_done, k_float, k_hi, k_lo, k_stacked = (sem(n) for n in (
            "k_done", "k_float", "k_hi", "k_lo", "k_stacked"))
        k_zero, k_spread = sem("k_zero"), sem("k_spread")
        v_done, v_float, v_hi, v_lo = (sem(n) for n in ("v_done", "v_float", "v_hi", "v_lo"))
        w_hi, w_lo = sem("w_hi"), sem("w_lo")
        w0_made, w2_made, w1_made = sem("w0_made"), sem("w2_made"), sem("w1_made")
        x_loaded, r_copied, out_stored = sem("x_loaded"), sem("r_copied"), sem("out_stored")
        var_ready, mv_ready, rstd_ready = sem("var_ready"), sem("mv_ready"), sem("rstd_ready")
        ln_step, xn_ready, xn_turned, xt_hi, xt_lo = (sem(n) for n in (
            "ln_step", "xn_ready", "xn_turned", "xt_hi", "xt_lo"))
        q_done, q_split, q_lo = sem("q_done"), sem("q_split"), sem("q_lo")
        q_stacked = [sem("q_stacked0"), sem("q_stacked1")]
        s_done, s_max, p_ready, p_turned, pt_hi, pt_lo = (sem(n) for n in (
            "s_done", "s_max", "p_ready", "p_turned", "pt_hi", "pt_lo"))
        pv_done, recip_done, pv_scaled, pv_added, attn_ready = (sem(n) for n in (
            "pv_done", "recip_done", "pv_scaled", "pv_added", "attn_ready"))
        c_turned, ct_hi, ct_lo, wo_done, xb_ready, x1_ready = (sem(n) for n in (
            "c_turned", "ct_hi", "ct_lo", "wo_done", "xb_ready", "x1_ready"))
        ffn_done, ffn_hi, ffn_lo, l2_done, out_ready = (sem(n) for n in (
            "ffn_done", "ffn_hi", "ffn_lo", "l2_done", "out_ready"))

        NX, NU, NT, NG, NF, NLN, NR = 2 * TT, U, TT, G, 2 * FT, 2 * TT, 1 + TT
        STACKS = 16 * 16
        STACK_USES = G // 2

        def nth(chunk, per_chunk, n):
            return chunk * per_chunk + (n + 1)

        tanh_x, tanh_f, _, fin_part, sgn0, _, h_scale, _, _, fin, wo_scale, abs0, abs1 = (
            c[:, n:n + 1] for n in range(13))

        def wait_apart(engine, semaphore, value):
            engine.wait_ge(semaphore, value)
            engine.nop(nofuse=True)

        block = es.enter_context(nc.Block())

        x_v = x.rearrange("(c p t) d -> c p (t d)", p=P, t=TT)
        out_v = out.rearrange("(c p t) d -> c p (t d)", p=P, t=TT)
        Y_flat = Y[:, :, :].rearrange("p t d -> p (t d)")
        X_flat = X.rearrange("p t d -> p (t d)")
        R_flat = R.rearrange("p t d -> p (t d)")

        @block.sync
        def _(sp):
            def load(to, source, semaphore):
                sp.dma_start(to, source).then_inc(semaphore, 16)

            def by_rows(w):
                return w.rearrange("(k p) n -> p k n", p=P)

            def to_all(v, n):
                return v.rearrange("(a n) -> a n", a=1).to_broadcast([P, n])

            load(ctx_f, ctx.rearrange("(b p) d -> p b d", p=P), ctx_in)
            load(Wk_f, by_rows(Wk), wk_in)
            with nc.allow_non_contiguous_dma(reason="two biases of 2 KiB, one feature per row"):
                load(bk_c[:, :], bk.rearrange("(k p) -> p k", p=P), bk_in)
                load(Y_flat, x_v[0], x_loaded)
                load(Wq_f, by_rows(Wq), wq_in)
                load(bq_c[:, :], bq.rearrange("(k p) -> p k", p=P), bq_in)
            load(Wv_f, by_rows(Wv), wv_in)
            load(bv_b[:, :], to_all(bv, D), bv_in)
            for n, s in enumerate((g_xattn, g_ffn, s0, s1, s2)):
                load(scal[:, n:n + 1], to_all(s, 1), scalars_in)
            load(bo_b[:, :], to_all(bo, D), bo_in)
            load(Wo_f, by_rows(Wo), wo_in)
            for half in range(2):
                for a in range(2):
                    load(k0_u[half][:, a].bitcast(u32), k0.rearrange("(a k p) (h n) -> a h p k n", a=2, p=P, h=2)[a, half],
                         k0_in[half])
            load(k2_u.bitcast(mybir.dt.uint32), by_rows(k2), k2_in)
            load(k1_u.bitcast(mybir.dt.uint32), by_rows(k1), k1_in)
            sp.wait_ge(s_done, NU)
            for r in range(4):
                for j in range(4):
                    sp.dma_start(
                        Kst[32 * r:32 * r + 32, j::4, :, :].rearrange("p m b n -> p m (b n)"),
                        KHL[32 * j:32 * j + 32, r // 2, :, :]).then_inc(k_stacked, 16)

            def stack_queries(a, g):
                wait_apart(sp, q_lo, nth(a, NG, g))
                wait_apart(sp, s_done, nth(a, NU, 4 * (g - 2) + 3))
                for r in range(4):
                    for j in range(4):
                        sp.dma_start(Qst[32 * r:32 * r + 32, g % 2, j, :],
                                     Qhl[32 * j:32 * j + 32, g % 2, r % 2, :])\
                          .then_inc(q_stacked[g % 2], 16)

            def keep_x1(a):
                wait_apart(sp, x1_ready, nth(a, NT, NT - 1))
                sp.dma_start(R_flat, X_flat).then_inc(r_copied, 16)

            def load_next(a):
                wait_apart(sp, xb_ready, nth(a, NT, NT - 1))
                sp.dma_start(Y_flat, x_v[a + 1]).then_inc(x_loaded, 16)

            def store(f):
                wait_apart(sp, out_ready, nth(f, NT, NT - 1))
                sp.dma_start(out_v[f], R_flat).then_inc(out_stored, 16)
                wait_apart(sp, out_stored, nth(f, 16, 15))

            load_next(0)
            sp.wait_ge(w0_made, KT)
            keep_x1(0)
            sp.wait_ge(w0_made, 2 * KT)
            for g in range(G):
                stack_queries(1, g)
            load_next(1)
            with sp.Fori(1, CHUNKS - 2) as i:
                store(i - 1)
                keep_x1(i)
                for g in range(G):
                    stack_queries(i + 1, g)
                load_next(i + 1)
            store(CHUNKS - 3)
            keep_x1(CHUNKS - 2)
            for g in range(G):
                stack_queries(CHUNKS - 1, g)
            store(CHUNKS - 2)
            keep_x1(CHUNKS - 1)
            for t in range(TT):
                sp.wait_ge(out_ready, nth(CHUNKS - 1, NT, t))
                sp.dma_start(out.rearrange("(c p t) d -> c p t d", p=P, t=TT)[CHUNKS - 1, :, t],
                             R[:, t, :]).then_inc(out_stored, 16)
            sp.wait_ge(out_stored, (CHUNKS - 1 + TT) * 16)

        @block.gpsimd
        def _(pool):
            pool.memset(ident[:, :], 0.0).then_inc(ident_zero, 1)
            pool.wait_ge(ident_zero, 1)
            pool.affine_select(out=ident[:, :], in_=ident[:, :], compare_op=ALU.not_equal, fill=1.0,
                               base=0, pattern=[[-1, P]], channel_multiplier=1).then_inc(ident_made, 1)
            pool.memset(halves[:, 0, :], -0.5).then_inc(half_made, 1)
            pool.memset(halves[:, 1, :], EPS).then_inc(half_made, 1)
            pool.memset(Kst[:, :, :, :], 0.0).then_inc(k_zero, 1)
            pool.memset(V[:, :, :, :], 1.0).then_inc(v_ones, 1)
            pool.memset(ones_mask[:, :], 0xbcbcbcbc).then_inc(masks_made, 1)
            pool.memset(eleventh_mask[:, :], 0x90909090).then_inc(masks_made, 1)

            def attend(item, a, first):
                kind, n = item
                if kind == "WO" or item == ("LN", TT - 1):
                    r, w = (0, slice(0, TT)) if kind == "LN" else (1 + n, slice(n, n + 1))
                    pool.wait_ge(mv_ready, nth(a, NR, r))
                    pool.tensor_tensor(var_eps[:, w], mv[:, w, 1], halves[:, 1, w], ALU.add)\
                        .then_inc(var_ready, 1)
                    pool.wait_ge(var_ready, nth(a, NR, r))
                    pool.tensor_tensor(rstd[:, w], var_eps[:, w], halves[:, 0, w], ALU.pow)\
                        .then_inc(rstd_ready, 1)
                if kind == "CT":
                    if n == 0 and first:
                        pool.wait_ge(const_step, 5)
                    if n == 0 and not first:
                        pool.wait_ge(r_copied, nth(a - 1, 16, 15))
                        pool.wait_ge(xn_ready, nth(a - 1, NX, NX - 1))
                    if n == 0:
                        pool.wait_ge(x_loaded, nth(a, 16, 15))
                    pool.tensor_tensor(X[:, n, :], Y[:, n, :], bo_b[:, :], ALU.add).then_inc(xb_ready, 1)
                if kind == "PV":
                    g, t = divmod(n, TT)
                    pool.wait_ge(pv_scaled, nth(a, NU, n))
                    heads = attn[:, t, g * P:(g + 1) * P].rearrange("p (j d) -> p j d", j=4)
                    high, low = pvs[:, n % 2, :, 0:HEAD], pvs[:, n % 2, :, HEAD:2 * HEAD]
                    if not first:
                        pool.tensor_tensor(heads, high, low, ALU.add).then_inc(attn_ready, 1)
                        return
                    pool.tensor_tensor(high, high, low, ALU.add).then_inc(pv_added, 1)
                    pool.wait_ge(pv_added, n + 1)
                    pool.wait_ge(recip_done, n + 1)
                    pool.tensor_tensor(
                        heads, high, rden[:, n % 2, :].rearrange("p (j o) -> p j o", o=1).to_broadcast([P, 4, HEAD]),
                        ALU.mult).then_inc(attn_ready, 1)

            pool.wait_ge(half_made, 2)
            for item in FIRST_ITEMS:
                attend(item, 0, True)
            for item in LOOP_ITEMS:
                attend(item, 1, False)
            for _, f0, f1 in LOOPS:
                with pool.Fori(f0, f1) as i:
                    for item in LOOP_ITEMS:
                        attend(item, i + 1, False)

        @block.scalar
        def _(act):
            def prepare(item):
                kind, n = item
                if kind == "K":
                    act.wait_ge(k_float, n + 1)
                    nc.scalar.activation(KHL[:, 0, n, :], Kf[n % 2], ACT.Copy).then_inc(k_hi, 1)
                if kind == "V":
                    act.wait_ge(v_float, n + 1)
                    act.wait_ge(v_ones, 1)
                    nc.scalar.activation(V[:, n, :, 0:HEAD], Vf[n].rearrange("p (h d) -> p h d", h=HEADS),
                                         ACT.Copy, scale=VS).then_inc(v_hi, 1)
                if kind == "CUT_Q":
                    act.wait_ge(wq_in, 16)
                    nc.scalar.activation(Wq_hi[:, n, :], Wq_f[:, n, :], ACT.Copy, scale=WS).then_inc(w_hi, 1)
                if kind == "CUT_O":
                    act.wait_ge(wo_in, 16)
                    nc.scalar.activation(Wo_hi[:, n, :], Wo_f[:, n, :], ACT.Copy, scale=WS).then_inc(w_hi, 1)
                if kind == "SCALARS":
                    act.wait_ge(scalars_in, 5 * 16)
                    nc.scalar.activation(c[:, 0:2], scal[:, 0:2], ACT.Tanh).then_inc(const_tanh, 1)
                if item == ("T2", 0):
                    act.wait_ge(w2_made, 1)

            def attend(item, a, first=False, second=False):
                kind, n = item
                if kind in ("T1", "T2"):
                    k = n + (TT if kind == "T2" else 0)
                    bank = (FIRST_BANK if first else LOOP_BANK)[item]
                    dst = xT_hi if kind == "T1" else hT_hi
                    act.wait_ge(xn_turned, nth(a, NX, k))
                    nc.scalar.activation(dst[:, :, n * P:(n + 1) * P],
                                         banks[bank][:, :].rearrange("p (k n) -> p k n", k=KT),
                                         ACT.Copy, scale=XS if kind == "T1" else h_scale)\
                        .then_inc(xt_hi, 1)
                if kind == "Q":
                    bank = banks[(FIRST_BANK if first else LOOP_BANK)[item]]
                    act.wait_ge(q_done, nth(a, NG, n))
                    if first and n == 0:
                        act.wait_ge(bq_in, 16)
                    if first and n >= 2:
                        act.wait_ge(s_done, 4 * (n - 2) + 4)
                    if second and n < 2:
                        act.wait_ge(s_done, 4 * (n + 2) + 4)
                    if not first and not (second and n < 2):
                        act.wait_ge(q_stacked[n % 2], ((a - 1) * STACK_USES + n // 2) * STACKS)
                    nc.scalar.activation(Qhl[:, n % 2, 0, :], bank[:, :], ACT.Identity,
                                         bias=bq_c[:, n:n + 1], scale=1 / (XS * WS))
                    if not (first and n == 0):
                        act.wait_ge(q_lo, nth(a, NG, n - 1))
                    nc.scalar.activation(Qf[:, :], bank[:, :], ACT.Identity, bias=bq_c[:, n:n + 1],
                                         scale=1 / (XS * WS)).then_inc(q_split, 1)
                if kind == "S":
                    bank = banks[(FIRST_BANK if first else LOOP_BANK)[item]]
                    act.wait_ge(s_max, nth(a, NU, n))
                    for j in range(4):
                        last = nc.scalar.activation(
                            Pf[:, n % 2, j * P:(j + 1) * P], bank[:, j * P:(j + 1) * P], ACT.Exp,
                            bias=nmax[:, n % 2, j:j + 1], scale=1.0)
                    last.then_inc(p_ready, 1)
                if kind == "T":
                    bank = banks[(FIRST_BANK if first else LOOP_BANK)[item]]
                    act.wait_ge(p_turned, nth(a, NU, n))
                    nc.scalar.activation(PT_hi[:, n % 2, :], bank[:, :], ACT.Copy, scale=PS)\
                        .then_inc(pt_hi, 1)
                if kind == "PV" and first:
                    act.wait_ge(recip_done, n + 1)
                    nc.scalar.activation(
                        pvs[:, n % 2, :, :],
                        banks[FIRST_BANK[item]][:, :].rearrange("p (j n) -> p j n", j=4)[:, :, 0:2 * HEAD],
                        ACT.Copy).then_inc(pv_scaled, 1)
                if kind == "CT":
                    bank = banks[(FIRST_BANK if first else LOOP_BANK)[item]]
                    act.wait_ge(c_turned, nth(a, NT, n))
                    nc.scalar.activation(cT_hi[:, n % 2, :], bank[:, :], ACT.Copy).then_inc(ct_hi, 1)

            def feed(slot, f):
                kind, n, q = slot
                if kind == "L0" or (kind == "L1" and q == 3):
                    e = n + (FT if kind == "L1" else 0)
                    dst = h0_hi[:, n, :] if kind == "L0" else h1_hi[:, n % 2, :]
                    act.wait_ge(ffn_done, nth(f, NF, e))
                    nc.scalar.activation(dst, banks[e % 2][:, :], ACT.Relu).then_inc(ffn_hi, 1)

            for item in ACT_FIRST_ITEMS:
                prepare(item)
                attend(item, 0, first=True)
            for s, slot in enumerate(SLOTS):
                if slot[0] == "L0" and slot[1] % 2 == 0:
                    act.wait_ge(w1_made, slot[1] + 2)
                feed(slot, 0)
                for item in WEAVE.get(s, ()):
                    attend(item, 1, second=True)
            for _, f0, f1 in LOOPS:
                with act.Fori(f0, f1) as i:
                    for s, slot in enumerate(SLOTS):
                        feed(slot, i)
                        for item in WEAVE.get(s, ()):
                            attend(item, i + 1)
            for slot in SLOTS:
                feed(slot, CHUNKS - 1)

        @block.vector
        def _(dve):
            V_ = nc.vector
            for b in range(BATCHES):
                dve.wait_ge(ctx_turned, b + 1)
                V_.tensor_copy(ctxT[:, :, b * P:(b + 1) * P],
                               banks[6 + b][:, :].rearrange("p (k n) -> p k n", k=KT))\
                    .then_inc(ctx_taken, 1)

            def follow_scalars():
                dve.wait_ge(scalars_in, 5 * 16)
                V_.tensor_scalar(c[:, 2:4], scal[:, 2:4], 0.0, None, ALU.is_ge).then_inc(const_step, 1)
                dve.wait_ge(const_step, 1)
                V_.tensor_scalar(c[:, 4:6], c[:, 2:4], 2.0, -1.0, ALU.mult, ALU.add).then_inc(const_step, 1)
                dve.wait_ge(const_step, 2)
                dve.wait_ge(const_tanh, 1)
                V_.tensor_scalar(h_scale, sgn0, XS, None, ALU.mult)
                V_.tensor_scalar(wo_scale, tanh_x, 1 / (VS * WS), None, ALU.mult)
                V_.tensor_scalar(fin_part, tanh_f, scal[:, 4:5], OUTS, ALU.mult, ALU.mult)
                V_.tensor_tensor(c[:, 11:13], scal[:, 2:4], c[:, 4:6], ALU.mult).then_inc(const_step, 1)
                dve.wait_ge(const_step, 3)
                V_.tensor_scalar(fin, fin_part, abs0, abs1, ALU.mult, ALU.mult)\
                    .then_inc(const_step, 1)
                dve.wait_ge(bo_in, 16)
                V_.tensor_scalar(bo_b[:, :], bo_b[:, :], tanh_x, None, ALU.mult).then_inc(const_step, 1)

            def words(w):
                w = w if len(w.shape) == 2 else w.rearrange("p k n -> p (k n)")
                return w.bitcast(u32)

            def follow_sign():
                sign_bits = w1_mask[:, :]
                V_.tensor_scalar(sign_bits, scal[:, 3:4].bitcast(u32), 31, 7, ALU.logical_shift_right,
                                 ALU.logical_shift_left).then_inc(const_step, 1)
                for n, shift in enumerate((8, 16)):
                    dve.wait_ge(const_step, 6 + n)
                    V_.scalar_tensor_tensor(out=sign_bits, in0=sign_bits, scalar=shift, in1=sign_bits,
                                            op0=ALU.logical_shift_left, op1=ALU.bitwise_or)\
                        .then_inc(const_step, 1)
                dve.wait_ge(const_step, 8)
                dve.wait_ge(masks_made, 2)
                V_.tensor_tensor(sign_bits, sign_bits, eleventh_mask[:, :], ALU.bitwise_xor)\
                    .then_inc(const_step, 1)
                dve.wait_ge(const_step, 9)

            def normalise(a, k, src, t, first):
                if not (first and k < 2):
                    dve.wait_ge(xn_turned, nth(a, NX, k - 2))
                V_.tensor_scalar(xn[:, k % 2, :], src, mv[:, t, 0:1], rstd[:, t:t + 1],
                                 ALU.subtract, ALU.mult).then_inc(xn_ready, 1)

            def attend(item, a, first):
                kind, n = item
                bank = banks[(FIRST_BANK if first else LOOP_BANK)[item]] if kind in ON_PE else None
                if kind == "LN":
                    if n == 0:
                        dve.wait_ge(x_loaded, nth(a, 16, 15))
                    V_.bn_stats(stats[:, n, :], Y[:, n, :]).then_inc(ln_step, 1)
                    if n == TT - 1:
                        wait_apart(dve, ln_step, nth(a, NLN, TT - 1))
                        for t in range(TT):
                            last = V_.bn_aggr(mv[:, t, :], stats[:, t, :])
                        last.then_inc(mv_ready, 1)
                if kind == "N1":
                    if n == 0:
                        dve.wait_ge(rstd_ready, nth(a, NR, 0))
                    normalise(a, n, Y[:, n, :], n, first)
                if kind in ("T1", "T2"):
                    k = n + (TT if kind == "T2" else 0)
                    hi, lo = (xT_hi, xT_lo) if kind == "T1" else (hT_hi, hT_lo)
                    dve.wait_ge(xt_hi, nth(a, NX, k))
                    V_.scalar_tensor_tensor(
                        out=lo[:, :, n * P:(n + 1) * P],
                        in0=bank[:, :].rearrange("p (k n) -> p k n", k=KT),
                        scalar=XS if kind == "T1" else h_scale, in1=hi[:, :, n * P:(n + 1) * P],
                        op0=ALU.mult, op1=ALU.subtract).then_inc(xt_lo, 1)
                if kind == "Q":
                    dve.wait_ge(q_split, nth(a, NG, n))
                    V_.tensor_tensor(Qhl[:, n % 2, 1, :], Qf[:, :], Qhl[:, n % 2, 0, :], ALU.subtract)\
                        .then_inc(q_lo, 1)
                if kind == "S":
                    dve.wait_ge(s_done, nth(a, NU, n))
                    V_.tensor_reduce(nmax[:, n % 2, :], bank[:, :].rearrange("p (j k) -> p j k", j=4),
                                     AX.X, ALU.max, negate=True).then_inc(s_max, 1)
                if kind == "T":
                    dve.wait_ge(pt_hi, nth(a, NU, n))
                    V_.scalar_tensor_tensor(out=PT_lo[:, n % 2, :], in0=bank[:, :], scalar=PS,
                                            in1=PT_hi[:, n % 2, :], op0=ALU.mult, op1=ALU.subtract)\
                        .then_inc(pt_lo, 1)
                if kind == "PV":
                    v = bank[:, :].rearrange("p (j n) -> p j n", j=4)
                    dve.wait_ge(pv_done, nth(a, NU, n))
                    if not (first and n < 2):
                        dve.wait_ge(attn_ready, nth(a, NU, n - 2))
                    V_.reciprocal(rden[:, n % 2, :], v[:, :, 2 * HEAD]).then_inc(recip_done, 1)
                    if first:
                        return
                    dve.wait_ge(recip_done, nth(a, NU, n))
                    V_.tensor_tensor(
                        pvs[:, n % 2, :, :], v[:, :, 0:2 * HEAD],
                        rden[:, n % 2, :].rearrange("p (j o) -> p j o", o=1).to_broadcast([P, 4, 2 * HEAD]),
                        ALU.mult).then_inc(pv_scaled, 1)
                if kind == "CT":
                    dve.wait_ge(ct_hi, nth(a, NT, n))
                    V_.tensor_tensor(cT_lo[:, n % 2, :], bank[:, :], cT_hi[:, n % 2, :], ALU.subtract)\
                        .then_inc(ct_lo, 1)
                if kind == "WO":
                    dve.wait_ge(wo_done, nth(a, NT, n))
                    dve.wait_ge(xb_ready, nth(a, NT, n))
                    V_.scalar_tensor_tensor(out=X[:, n, :], in0=bank[:, :], scalar=wo_scale,
                                            in1=X[:, n, :], op0=ALU.mult, op1=ALU.add)\
                        .then_inc(x1_ready, 1)
                    dve.wait_ge(x1_ready, nth(a, NT, n))
                    V_.bn_stats(stats[:, n, :], X[:, n, :]).then_inc(ln_step, 1)
                    wait_apart(dve, ln_step, nth(a, NLN, TT + n))
                    V_.bn_aggr(mv[:, n, :], stats[:, n, :]).then_inc(mv_ready, 1)
                if kind == "N2":
                    dve.wait_ge(rstd_ready, nth(a, NR, 1 + n))
                    normalise(a, TT + n, X[:, n, :], n, first)

            def feed(slot, f):
                kind, n, q = slot
                if kind == "L0" or (kind == "L1" and q == 3):
                    e = n + (FT if kind == "L1" else 0)
                    hi, lo = (h0_hi[:, n, :], h0_lo[:, n, :]) if kind == "L0" else (
                        h1_hi[:, n % 2, :], h1_lo[:, n % 2, :])
                    dve.wait_ge(ffn_hi, nth(f, NF, e))
                    V_.scalar_tensor_tensor(out=lo, in0=banks[e % 2][:, :], scalar=0.0, in1=hi,
                                            op0=ALU.max, op1=ALU.subtract).then_inc(ffn_lo, 1)
                if kind == "L2" and n == FT - 1:
                    dve.wait_ge(r_copied, nth(f, 16, 15))
                    for t in range(TT):
                        dve.wait_ge(l2_done, nth(f, NT, t))
                        V_.scalar_tensor_tensor(out=R[:, t, :], in0=banks[2 + t][:, :], scalar=fin,
                                                in1=R[:, t, :], op0=ALU.mult, op1=ALU.add)\
                            .then_inc(out_ready, 1)

            def prepare(item):
                kind, n = item
                if kind == "K":
                    if n == 0:
                        dve.wait_ge(bk_in, 16)
                    dve.wait_ge(k_done, n + 1)
                    if n >= 2:
                        dve.wait_ge(k_lo, n - 1)
                    V_.tensor_scalar(Kf[n % 2], banks[n][:, 0:BATCHES * P], bk_c[:, n:n + 1], SCALE,
                                     ALU.add, ALU.mult).then_inc(k_float, 1)
                    dve.wait_ge(k_hi, n + 1)
                    V_.tensor_tensor(KHL[:, 1, n, :], Kf[n % 2], KHL[:, 0, n, :], ALU.subtract)\
                        .then_inc(k_lo, 1)
                if kind == "SPREAD":
                    dve.wait_ge(k_zero, 1)
                    dve.wait_ge(k_lo, KT)
                    for j in range(4):
                        rows = slice(HEAD * j, HEAD * j + HEAD)
                        V_.tensor_copy(Kst[rows, j::4, :, :],
                                       KHL[rows, :, :, 0:P].rearrange("p a m n -> p m a n"))\
                            .then_inc(k_spread, 1)
                if kind == "V":
                    if n == 0:
                        dve.wait_ge(bv_in, 16)
                    dve.wait_ge(v_done, n + 1)
                    V_.tensor_tensor(Vf[n], banks[4 + n][:, :], bv_b[:, :], ALU.add).then_inc(v_float, 1)
                    dve.wait_ge(v_hi, n + 1)
                    V_.scalar_tensor_tensor(
                        out=V[:, n, :, HEAD:2 * HEAD], in0=Vf[n].rearrange("p (h d) -> p h d", h=HEADS),
                        scalar=VS, in1=V[:, n, :, 0:HEAD], op0=ALU.mult, op1=ALU.subtract)\
                        .then_inc(v_lo, 1)
                if kind == "CUT_Q":
                    dve.wait_ge(w_hi, n + 1)
                    V_.scalar_tensor_tensor(out=Wq_lo[:, n, :], in0=Wq_f[:, n, :], scalar=WS,
                                            in1=Wq_hi[:, n, :], op0=ALU.mult, op1=ALU.subtract)\
                        .then_inc(w_lo, 1)
                if kind == "CUT_O":
                    dve.wait_ge(w_hi, KT + n + 1)
                    V_.scalar_tensor_tensor(out=Wo_lo[:, n, :], in0=Wo_f[:, n, :], scalar=WS,
                                            in1=Wo_hi[:, n, :], op0=ALU.mult, op1=ALU.subtract)\
                        .then_inc(w_lo, 1)
                if kind == "SCALARS":
                    follow_scalars()
                    follow_sign()
                if kind == "W0":
                    half, k = divmod(n, KT)
                    if k == 0:
                        dve.wait_ge(k0_in[half], 32)
                    V_.tensor_tensor(W0[:, k, half * F // 2:(half + 1) * F // 2], k0_u[half][:, 0, k, :],
                                     k0_u[half][:, 1, k, :], ALU.subtract, saturate=False)\
                        .then_inc(w0_made, 1)
                if kind == "W2":
                    dve.wait_ge(k2_in, 16)
                    dve.wait_ge(masks_made, 2)
                    V_.tensor_scalar(words(W2[:, :, :]), k2_u.bitcast(u32).rearrange("p k n -> p (k n)"), 7,
                                     ones_mask[:, :], ALU.logical_shift_left, ALU.bitwise_xor)\
                        .then_inc(w2_made, 1)
                if kind == "W1":
                    if n == 0:
                        dve.wait_ge(k1_in, 16)
                    for k in (n, FT // 2 + n):
                        V_.tensor_scalar(words(W1[:, k, :]), k1_u[:, k, :].bitcast(u32), 7, w1_mask[:, :],
                                         ALU.logical_shift_left, ALU.bitwise_xor).then_inc(w1_made, 1)
                if item == ("T2", 0):
                    dve.wait_ge(w2_made, 1)

            for item in FIRST_ITEMS:
                prepare(item)
                attend(item, 0, True)
            for s, slot in enumerate(SLOTS):
                feed(slot, 0)
                if s in LATE_WEIGHTS:
                    prepare(LATE_WEIGHTS[s])
                for item in WEAVE.get(s, ()):
                    attend(item, 1, False)
            for _, f0, f1 in LOOPS:
                with dve.Fori(f0, f1) as i:
                    for s, slot in enumerate(SLOTS):
                        feed(slot, i)
                        for item in WEAVE.get(s, ()):
                            attend(item, i + 1, False)
            for slot in SLOTS:
                feed(slot, CHUNKS - 1)

        @block.tensor
        def _(pe):
            mm, turn = nc.tensor.matmul, nc.tensor.transpose
            pe.wait_ge(ident_made, 1)
            pe.wait_ge(ctx_in, 16)
            for b in range(BATCHES):
                for k in range(KT):
                    last = turn(banks[6 + b][:, k * P:(k + 1) * P], ctx_f[:, b, k * P:(k + 1) * P],
                                ident[:, :])
                last.then_inc(ctx_turned, 1)
            pe.wait_ge(ctx_taken, BATCHES)
            pe.wait_ge(wk_in, 16)

            def prepare(item):
                kind, n = item
                if kind == "K":
                    if n == 0:
                        pe.wait_ge(wk_in, 16)
                    for k in range(KT):
                        last = mm(banks[n][:, 0:BATCHES * P], Wk_f[:, k, n * P:(n + 1) * P], ctxT[:, k, :],
                                  start=k == 0, stop=k == KT - 1)
                    last.then_inc(k_done, 1)
                if kind == "V":
                    if n == 0:
                        pe.wait_ge(wv_in, 16)
                    for k in range(KT):
                        last = mm(banks[4 + n][:, :], ctxT[:, k, n * P:(n + 1) * P], Wv_f[:, k, :],
                                  start=k == 0, stop=k == KT - 1)
                    last.then_inc(v_done, 1)
                if item == ("Q", 0):
                    pe.wait_ge(w_lo, KT)
                    pe.wait_ge(k_lo, KT)
                if item == ("S", 0):
                    pe.wait_ge(k_spread, 4)
                if item in (("PV", 0), ("PV", 1)):
                    pe.wait_ge(v_lo, item[1] + 1)
                if item == ("WO", 0):
                    pe.wait_ge(w_lo, 2 * KT)

            def released(item, a):
                kind, n = item
                return {"T1": (xt_lo, NX, n), "T2": (xt_lo, NX, TT + n), "Q": (q_split, NG, n),
                        "S": (p_ready, NU, n), "T": (pt_lo, NU, n), "PV": (pv_scaled, NU, n),
                        "CT": (ct_lo, NT, n), "WO": (x1_ready, NT, n)}[kind]

            def attend(item, a, batch, first):
                kind, n = item
                if kind not in ON_PE:
                    return
                if first:
                    bank, before, since = FIRST_BANK[item], user_before(FIRST_ITEMS, FIRST_BANK, item), a
                else:
                    bank, before, since = LOOP_BANK[item], user_before(LOOP_ITEMS, LOOP_BANK, item), a
                    if before is None:
                        before, since = [i for i in LOOP_ITEMS if LOOP_BANK.get(i) == bank][-1], a - 1
                if before is not None:
                    signal, per_chunk, m = released(before, a)
                    pe.wait_ge(signal, nth(since, per_chunk, m))
                bank = banks[bank]
                if kind in ("T1", "T2"):
                    k = n + (TT if kind == "T2" else 0)
                    pe.wait_ge(xn_ready, nth(a, NX, k))
                    for d in range(KT):
                        last = turn(bank[:, d * P:(d + 1) * P], xn[:, k % 2, d * P:(d + 1) * P],
                                    ident[:, :])
                    last.then_inc(xn_turned, 1)
                if kind == "Q":
                    if n == 0:
                        pe.wait_ge(xt_lo, nth(a, NX, TT - 1))
                    for k in range(KT):
                        w_h, w_l = (w[:, k, n * P:(n + 1) * P] for w in (Wq_hi, Wq_lo))
                        mm(bank[:, :], w_h, xT_hi[:, k, :], start=k == 0, stop=False)
                        mm(bank[:, :], w_h, xT_lo[:, k, :], start=False, stop=False)
                        last = mm(bank[:, :], w_l, xT_hi[:, k, :], start=False, stop=k == KT - 1)
                    last.then_inc(q_done, 1)
                if kind == "S":
                    g, t = divmod(n, TT)
                    if first:
                        if t == 0:
                            pe.wait_ge(q_lo, g + 1)
                        for part in range(4):
                            last = mm(bank[:, :], Qhl[:, g % 2, part % 2, t * P:(t + 1) * P],
                                      Kst[:, 4 * g:4 * g + 4, part // 2, :],
                                      start=part == 0, stop=part == 3)
                        last.then_inc(s_done, 1)
                        return
                    if t == 0:
                        pe.wait_ge(q_stacked[g % 2], ((a - 1) * STACK_USES + g // 2 + 1) * STACKS)
                    for j in range(4):
                        last = mm(bank[:, j * P:(j + 1) * P], Qst[:, g % 2, j, t * P:(t + 1) * P],
                                  Kst[:, 4 * g + j, batch, :], start=True, stop=True)
                    last.then_inc(s_done, 1)
                if kind == "T":
                    pe.wait_ge(p_ready, nth(a, NU, n))
                    for j in range(4):
                        last = turn(bank[:, j * P:(j + 1) * P], Pf[:, n % 2, j * P:(j + 1) * P],
                                    ident[:, :])
                    last.then_inc(p_turned, 1)
                if kind == "PV":
                    g, t = divmod(n, TT)
                    pe.wait_ge(pt_lo, nth(a, NU, n))
                    for j in range(4):
                        o, v = bank[:, j * P:j * P + VW - 1], V[:, batch, 4 * g + j, 0:VW - 1]
                        mm(o, PT_hi[:, n % 2, j * P:(j + 1) * P], v, start=True, stop=False)
                        last = mm(o, PT_lo[:, n % 2, j * P:(j + 1) * P], v, start=False, stop=True)
                    last.then_inc(pv_done, 1)
                if kind == "CT":
                    pe.wait_ge(attn_ready, nth(a, NU, (G - 1) * TT + n))
                    for k in range(KT):
                        last = turn(bank[:, k * P:(k + 1) * P], attn[:, n, k * P:(k + 1) * P],
                                    ident[:, :])
                    last.then_inc(c_turned, 1)
                if kind == "WO":
                    pe.wait_ge(ct_lo, nth(a, NT, n))
                    for k in range(KT):
                        c_h, c_l = (w[:, n % 2, k * P:(k + 1) * P] for w in (cT_hi, cT_lo))
                        mm(bank[:, :], c_h, Wo_hi[:, k, :], start=k == 0, stop=False)
                        mm(bank[:, :], c_h, Wo_lo[:, k, :], start=False, stop=False)
                        last = mm(bank[:, :], c_l, Wo_hi[:, k, :], start=False, stop=k == KT - 1)
                    last.then_inc(wo_done, 1)

            def feed(slot, f):
                kind, n, q = slot
                if kind == "L0":
                    if n == 0:
                        wait_apart(pe, xt_lo, nth(f, NX, NX - 1))
                    if n >= 2:
                        wait_apart(pe, ffn_lo, nth(f, NF, n - 2))
                    for k in range(KT):
                        w = W0[:, k, n * P:(n + 1) * P]
                        mm(banks[n % 2][:, :], w, hT_hi[:, k, :], start=k == 0, stop=False)
                        last = mm(banks[n % 2][:, :], w, hT_lo[:, k, :], start=False, stop=k == KT - 1)
                    last.then_inc(ffn_done, 1)
                if kind == "L1":
                    if q == 0:
                        wait_apart(pe, ffn_lo, nth(f, NF, FT + n - 2))
                    if n == 0:
                        wait_apart(pe, ffn_lo, nth(f, NF, 4 * q + 3))
                    for k in range(4 * q, 4 * q + 4):
                        w = W1[:, k, n * P:(n + 1) * P]
                        mm(banks[n % 2][:, :], w, h0_hi[:, k, :], start=k == 0, stop=False)
                        last = mm(banks[n % 2][:, :], w, h0_lo[:, k, :], start=False, stop=k == FT - 1)
                    if q == 3:
                        last.then_inc(ffn_done, 1)
                if kind == "L2":
                    wait_apart(pe, ffn_lo, nth(f, NF, FT + n))
                    for t in range(TT):
                        tok = slice(t * P, (t + 1) * P)
                        mm(banks[2 + t][:, :], h1_hi[:, n % 2, tok], W2[:, n, :],
                           start=n == 0, stop=False)
                        last = mm(banks[2 + t][:, :], h1_lo[:, n % 2, tok], W2[:, n, :],
                                  start=False, stop=n == FT - 1)
                        if n == FT - 1:
                            last.then_inc(l2_done, 1)

            for item in FIRST_ITEMS:
                prepare(item)
                attend(item, 0, 0, True)
            pe.wait_ge(k_stacked, 16 * 16)
            pe.wait_ge(w0_made, KT)
            pe.wait_ge(w2_made, 1)
            for s, slot in enumerate(SLOTS):
                if slot == ("L0", FT // 2, 0):
                    pe.wait_ge(w0_made, 2 * KT)
                if slot == ("L1", 0, 0):
                    pe.wait_ge(w1_made, FT)
                feed(slot, 0)
                for item in WEAVE.get(s, ()):
                    attend(item, 1, 0, False)
            for batch, f0, f1 in LOOPS:
                with pe.Fori(f0, f1) as i:
                    for s, slot in enumerate(SLOTS):
                        feed(slot, i)
                        for item in WEAVE.get(s, ()):
                            attend(item, i + 1, batch, False)
            for slot in SLOTS:
                feed(slot, CHUNKS - 1)


_INS = ["x", "ctx_1024", "g_xattn", "g_ffn", "L0_xattn_Wq", "L0_xattn_Wk", "L0_xattn_Wv", "L0_xattn_Wo",
        "L0_xattn_bq", "L0_xattn_bk", "L0_xattn_bv", "L0_xattn_bo", "L0_ffn_k0", "L0_ffn_k1",
        "L0_ffn_k2", "L0_ffn_s0", "L0_ffn_s1", "L0_ffn_s2"]


def kernel(**inputs):
    import numpy as _np
    import concourse.bacc as _bacc
    from concourse import mybir as _mybir
    from concourse.bass_utils import run_bass_kernel_spmd as _run

    nc = _bacc.Bacc("TRN2", target_bir_lowering=False, num_devices=1)
    arrays, args = {}, []
    for name in _INS:
        a = _np.ascontiguousarray(inputs[name])
        if a.ndim == 3:
            a = a.reshape(-1, a.shape[-1])
        if a.ndim == 0:
            a = a.reshape(1)
        if a.dtype == _np.bool_:
            a = a.view(_np.uint32)
        arrays[f"in_{name}_dram"] = a
        args.append(nc.dram_tensor(f"in_{name}_dram", a.shape, _mybir.dt.from_np(a.dtype),
                                   kind="ExternalInput").ap())
    shape = inputs["x"].shape
    out = nc.dram_tensor("out_dram", (shape[0] * shape[1], shape[2]), _mybir.dt.float32,
                         kind="ExternalOutput").ap()
    gated_block_kernel(nc, *args, out)
    r = _run(nc, [arrays], core_ids=[0])
    return r.results[0]["out_dram"].reshape(shape)
```
